# Optimizing a Trainium2 kernel written in Bass

```python
import numpy as np
import jax
import jax.numpy as jnp

def _softmax(x, axis=-1):
    return jax.nn.softmax(x, axis=axis)

def _gelu(x):
    return jax.nn.gelu(x, approximate=True)

def _silu(x):
    return jax.nn.silu(x)

def _sigmoid(x):
    return jax.nn.sigmoid(x)

def _layernorm(x, axis=-1, eps=1e-05):
    m = jnp.mean(x, axis=axis, keepdims=True)
    v = jnp.var(x, axis=axis, keepdims=True)
    return (x - m) / jnp.sqrt(v + eps)

def _scatter_add(tgt, idx, src, axis=0):
    return tgt.at[idx].add(src)

def _segment_sum(src, seg, n):
    return jax.ops.segment_sum(src, seg, n)
kernel_name = 'mk_prb_d1_jaxref_r8_612c96'

def setup_inputs(seed: int=0):
    np.random.seed(seed)
    _w = jnp.asarray

    def _L0_attn_setup():
        import jax, jax.numpy as jnp
        import numpy as np
        DIM = 128
        STATE = 128
        BATCH, SEQ = (4, 512)
        key = jax.random.key(seed)
        ks = jax.random.split(key, 12)
        s = 1.0 / np.sqrt(DIM)
        s4 = 1.0 / np.sqrt(DIM // 4)
        ss = 1.0 / np.sqrt(STATE)
        inp = {'x': jax.random.normal(ks[0], (BATCH, SEQ, DIM), dtype=jnp.float32), 'W_B': jax.random.uniform(ks[1], (DIM, STATE), minval=-s, maxval=s), 'b_B': jax.random.uniform(ks[2], (STATE,), minval=-s, maxval=s), 'W_C': jax.random.uniform(ks[3], (DIM, STATE), minval=-s, maxval=s), 'b_C': jax.random.uniform(ks[4], (STATE,), minval=-s, maxval=s), 'W_dt1': jax.random.uniform(ks[5], (DIM, DIM // 4), minval=-s, maxval=s), 'b_dt1': jax.random.uniform(ks[6], (DIM // 4,), minval=-s, maxval=s), 'W_dt2': jax.random.uniform(ks[7], (DIM // 4, STATE), minval=-s4, maxval=s4), 'b_dt2': jnp.full((STATE,), -4.0, dtype=jnp.float32), 'omega_base': jax.random.normal(ks[8], (STATE,)) * 0.1, 'D': jnp.ones((DIM,), dtype=jnp.float32), 'W_out': jax.random.uniform(ks[9], (STATE, DIM), minval=-ss, maxval=ss), 'b_out': jax.random.uniform(ks[10], (DIM,), minval=-ss, maxval=ss)}
        return inp
    _L0_attn_in = _L0_attn_setup()

    def _L0_ffn_setup():
        import jax, jax.numpy as jnp
        import numpy as np
        D_MODEL = 128
        D_FF = 512
        N_EXPERTS = 8
        TOP_K = 2
        key = jax.random.key(seed)
        ks = jax.random.split(key, 8)
        s = 1.0 / np.sqrt(D_MODEL)
        sf = 1.0 / np.sqrt(D_FF)
        return {'x': jax.random.normal(ks[0], (4, 128, D_MODEL), dtype=jnp.float32), 'W1': jax.random.uniform(ks[1], (N_EXPERTS, D_MODEL, D_FF), jnp.float32, -s, s), 'b1': jax.random.uniform(ks[2], (N_EXPERTS, D_FF), jnp.float32, -s, s), 'W2': jax.random.uniform(ks[3], (N_EXPERTS, D_FF, D_MODEL), jnp.float32, -sf, sf), 'b2': jax.random.uniform(ks[4], (N_EXPERTS, D_MODEL), jnp.float32, -sf, sf), 'Wg': jax.random.uniform(ks[5], (D_MODEL, N_EXPERTS), jnp.float32, -s, s), 'bg': jax.random.uniform(ks[6], (N_EXPERTS,), jnp.float32, -s, s)}
    _L0_ffn_in = _L0_ffn_setup()
    _d = {'L0_attn_x': _L0_attn_in['x'], 'L0_attn_W_B': _L0_attn_in['W_B'], 'L0_attn_b_B': _L0_attn_in['b_B'], 'L0_attn_W_C': _L0_attn_in['W_C'], 'L0_attn_b_C': _L0_attn_in['b_C'], 'L0_attn_W_dt1': _L0_attn_in['W_dt1'], 'L0_attn_b_dt1': _L0_attn_in['b_dt1'], 'L0_attn_W_dt2': _L0_attn_in['W_dt2'], 'L0_attn_b_dt2': _L0_attn_in['b_dt2'], 'L0_attn_omega_base': _L0_attn_in['omega_base'], 'L0_attn_D': _L0_attn_in['D'], 'L0_attn_W_out': _L0_attn_in['W_out'], 'L0_attn_b_out': _L0_attn_in['b_out'], 'L0_ffn_W1': _L0_ffn_in['W1'], 'L0_ffn_b1': _L0_ffn_in['b1'], 'L0_ffn_W2': _L0_ffn_in['W2'], 'L0_ffn_b2': _L0_ffn_in['b2'], 'L0_ffn_Wg': _L0_ffn_in['Wg'], 'L0_ffn_bg': _L0_ffn_in['bg']}
    _x0 = _d['L0_attn_x']
    _d['L0_attn_x'] = jax.random.normal(jax.random.fold_in(jax.random.key(seed), 1), (16, 512, 128), dtype=_x0.dtype)
    del _x0
    return _d

def reference(L0_attn_x, L0_attn_W_B, L0_attn_b_B, L0_attn_W_C, L0_attn_b_C, L0_attn_W_dt1, L0_attn_b_dt1, L0_attn_W_dt2, L0_attn_b_dt2, L0_attn_omega_base, L0_attn_D, L0_attn_W_out, L0_attn_b_out, L0_ffn_W1, L0_ffn_b1, L0_ffn_W2, L0_ffn_b2, L0_ffn_Wg, L0_ffn_bg):

    def _L0_attn_ref(x, W_B, b_B, W_C, b_C, W_dt1, b_dt1, W_dt2, b_dt2, omega_base, D, W_out, b_out):
        import jax, jax.numpy as jnp
        import numpy as np
        DIM = 128
        STATE = 128
        BATCH, SEQ = (4, 512)
        Bm = x @ W_B + b_B
        Cm = x @ W_C + b_C
        dt = jax.nn.softplus((x @ W_dt1 + b_dt1) @ W_dt2 + b_dt2)
        omega = omega_base * dt
        phi = jnp.cumsum(omega, axis=1)
        content = Bm * x[..., :STATE]
        cphi, sphi = (jnp.cos(phi), jnp.sin(phi))
        memory_real = jnp.cumsum(content * cphi, axis=1)
        memory_imag = jnp.cumsum(content * sphi, axis=1)
        retrieved = Cm * (memory_real * cphi + memory_imag * sphi)
        y = retrieved @ W_out + b_out + D * x
        return y

    def _L0_ffn_ref(x, W1, b1, W2, b2, Wg, bg):
        import jax, jax.numpy as jnp
        import numpy as np
        D_MODEL = 128
        D_FF = 512
        N_EXPERTS = 8
        TOP_K = 2
        logits = jnp.einsum('bsd,de->bse', x, Wg) + bg
        probs = jax.nn.softmax(logits, axis=-1)
        topk_vals, topk_idx = jax.lax.top_k(probs, TOP_K)
        mask = jax.nn.one_hot(topk_idx, N_EXPERTS, dtype=probs.dtype).sum(axis=-2)
        probs = probs * mask
        denom = probs.sum(axis=-1, keepdims=True)
        denom = denom + (denom == 0).astype(probs.dtype)
        probs = probs / denom
        h = jnp.einsum('bsd,edf->besf', x, W1) + b1[None, :, None, :]
        h = jax.nn.gelu(h, approximate=False)
        y = jnp.einsum('besf,efd->besd', h, W2) + b2[None, :, None, :]
        out = jnp.einsum('bse,besd->bsd', probs, y)
        return out
    x = L0_attn_x
    xn = _layernorm(x, axis=-1)
    x = x + _L0_attn_ref(xn, L0_attn_W_B, L0_attn_b_B, L0_attn_W_C, L0_attn_b_C, L0_attn_W_dt1, L0_attn_b_dt1, L0_attn_W_dt2, L0_attn_b_dt2, L0_attn_omega_base, L0_attn_D, L0_attn_W_out, L0_attn_b_out) + _L0_ffn_ref(xn, L0_ffn_W1, L0_ffn_b1, L0_ffn_W2, L0_ffn_b2, L0_ffn_Wg, L0_ffn_bg)
    return x

_drawn_inputs = setup_inputs


def setup_inputs(seed=0):
    import zlib

    import numpy as np

    out = dict(_drawn_inputs(seed))
    spreads = {'L0_attn_b_dt2': (-4.0, 0.2), 'L0_attn_D': (1.0, 0.2)}
    factors = {'L0_attn_W_dt1': 7.98,
     'L0_attn_b_dt1': 7.626,
     'L0_attn_W_dt2': 4.89,
     'L0_attn_b_out': 5.846,
     'L0_ffn_b1': 8.0,
     'L0_ffn_b2': 8.0,
     'L0_ffn_Wg': 2.67,
     'L0_ffn_bg': 8.0}
    for name, (base, spread) in spreads.items():
        noise = np.random.default_rng([zlib.crc32(name.encode()), seed]).standard_normal(out[name].shape)
        drawn = base * np.exp(spread * noise) if base else spread * noise
        out[name] = jnp.asarray(drawn.astype(out[name].dtype))
    for name, factor in factors.items():
        out[name] = (out[name] * factor).astype(out[name].dtype)
    return out
```

```python
from contextlib import ExitStack

import concourse.bass as bass
from concourse import mybir

ALU = mybir.AluOpType
ACT = mybir.ActivationFunctionType
F32 = mybir.dt.float32
F16 = mybir.dt.float16
BF16 = mybir.dt.bfloat16
I32 = mybir.dt.int32
U32 = mybir.dt.uint32
AX = mybir.AxisListType.X
RMAX = bass.bass_isa.ReduceOp.max

P = 128
B, SEQ, D = 16, 512, 128
TOK = B * SEQ
TPB = SEQ // P
T = B * TPB
E, FF, K = 8, 512, 2
CH = FF // P
RANK = 32
TILE = 256
HALF = TILE // P
N_TILES = K * TOK // TILE + E - 1
ROWS = N_TILES * TILE
ROW = D + 1
NOWHERE = 65535
ROUND = 1.5 * 2.0 ** 23
TWO_PI = 6.283185
U = 4


def need(eng, sem, count):
    if isinstance(count, int) and count <= 0:
        return
    eng.wait_ge(sem, count)


def steps(eng, n, body, unroll=U):
    for q in range(unroll):
        body(0, q)
    with eng.Fori(1, n // unroll) as k:
        for q in range(unroll):
            body(k, q)
    for j in range(n // unroll * unroll, n):
        body(j // unroll, j % unroll)


def program(nc, x, W_B, b_B, W_C, b_C, W_dt1, b_dt1, W_dt2, b_dt2, omega, D_skip, W_out, b_out,
            W1, b1, W2, b2, Wg, bg, out):
    with ExitStack() as ctx:
        def sb(name, shape, dt=F32):
            return ctx.enter_context(nc.sbuf_tensor(name, shape, dt))

        def sem(name):
            return ctx.enter_context(nc.semaphore(name))

        grouped = nc.dram_tensor("grouped", (ROWS, ROW), F32, kind="Internal").ap()
        expert_out = nc.dram_tensor("expert_out", (K * TOK, D), F32, kind="Internal").ap()

        x_seq = x.rearrange("(b p j) d -> p b j d", p=P, j=TPB)
        out_seq = out.rearrange("(b p j) d -> p b j d", p=P, j=TPB)
        eo_seq = expert_out.rearrange("(c b p j) d -> p c b j d", p=P, j=TPB, c=K)

        ps = ctx.enter_context(nc.psum_tensor("ps", [P, 8, 512], F32))

        acc = sb("acc", [P, T, D])
        row = sb("row", [P, T, ROW])
        xnT = sb("xnT", [P, B, SEQ])
        shared = sb("shared", [P, B * SEQ])
        w1h = sb("w1h", [P, E * FF], F16)
        w1l = sb("w1l", [P, E * FF], F16)
        w2h = sb("w2h", [P, E * FF], F16)
        w2l = sb("w2l", [P, E * FF], F16)
        ident = sb("ident", [P, P])
        row0 = sb("row0", [P, P])
        before = sb("before", [P, P], BF16)
        ones16 = sb("ones16", [P, P], BF16)
        wB = sb("wB", [P, D])
        wC = sb("wC", [P, D])
        wO = sb("wO", [P, D])
        wG = sb("wG", [P, E])
        wdt1 = sb("wdt1", [P, RANK])
        wdt1T = sb("wdt1T", [RANK, P])
        wdt2 = sb("wdt2", [RANK, P])
        wdt = sb("wdt", [P, P])
        cols = sb("cols", [P, 8])
        bout = sb("bout", [P, D])
        dskip = sb("dskip", [P, D])
        bgate = sb("bgate", [P, E])
        b1rows = sb("b1rows", [E * CH, P])
        b1T = sb("b1T", [P, E * CH])
        b2diag = sb("b2diag", [P, TPB, D])
        pT = sb("pT", [P, U, P])
        pTs = sb("pTs", [P, P])
        padrow = sb("padrow", [P, ROW])
        absw = sb("absw", [P, 2])
        maxw = sb("maxw", [P, 2])
        pw = sb("pw", [P, 2])
        scl = sb("scl", [P, 8])
        xn2 = sb("xn2", [P, 2, TPB, D])
        xnT2 = sb("xnT2", [P, 2, SEQ])
        stats = sb("stats", [P, 2, TPB, 6])
        mv = sb("mv", [P, 2, TPB, 2])
        rstd = sb("rstd", [P, 2, TPB])
        vare = sb("vare", [P, 2, TPB])
        minus_half = sb("minus_half", [P, TPB])
        dx = sb("dx", [P, TPB, D])
        lg = sb("lg", [P, T, E])
        pr = sb("pr", [P, T, E])
        gw = sb("gw", [P, T, E])
        g1 = sb("g1", [P, T, E])
        g2 = sb("g2", [P, T, E])
        mask16 = sb("mask16", [P, T, E], BF16)
        mx = sb("mx", [P, T])
        sm = sb("sm", [P, T])
        m12 = sb("m12", [P, K, T])
        gk = sb("gk", [P, K, T])
        den = sb("den", [P, T])
        den0 = sb("den0", [P, T])
        pos = sb("pos", [P, K, T], I32)
        posf = sb("posf", [P, K, T])
        desc = sb("desc", [P, E])
        jrow = sb("jrow", [P, N_TILES])
        tot, cum = (xn2[:, u].rearrange("p j d -> p (j d)").rearrange("p (e t) -> p e t", e=E) for u in range(2))
        zeros = sb("zeros", [P, SEQ])
        sizes = sb("sizes", [P, 8, E])
        past = xnT2[:].rearrange("p u s -> p (u s)")[:, 0:N_TILES * E].rearrange("p (n e) -> p n e", e=E)
        tile_e = sb("tile_e", [P, N_TILES])
        tile_expert = sb("tile_expert", [P, N_TILES], I32)
        def flat(v):
            return v[:].rearrange("p a b -> p (a b)")

        absz, relz = xn2[:].rearrange("p u j d -> p u (j d)"), xnT2
        ex = sb("ex", [P, 2, SEQ])
        lnz = sb("lnz", [P, 2, SEQ])
        ret = lnz
        steps_sum = flat(dx)
        turns, whole = flat(pr), flat(gw)
        sn, ab, cs = absz, relz, ex
        content, p1, m1 = flat(g1), flat(g2), flat(lg)
        p2, m2 = turns, steps_sum
        q1, q2, qs = m1, m2, content

        at = [0]

        def cut(n, dt=F32):
            words = n * (2 if dt == F16 else 4) // 4
            v = shared[:, at[0]:at[0] + words]
            at[0] += words
            return v.bitcast(dt) if dt != F32 else v

        xs = [cut(HALF * ROW).rearrange("p (h c) -> p h c", h=HALF) for _ in range(U)]
        xh = [cut(TILE, F16) for _ in range(2)]
        xl = [cut(TILE, F16) for _ in range(2)]
        gel = [cut(CH * TILE).rearrange("p (c n) -> p c n", c=CH) for _ in range(2)]
        hh = [cut(CH * TILE, F16).rearrange("p (c n) -> p c n", c=CH) for _ in range(2)]
        hl = [cut(CH * TILE, F16).rearrange("p (c n) -> p c n", c=CH) for _ in range(2)]
        ysb = [cut(HALF * D).rearrange("p (h d) -> p h d", h=HALF) for _ in range(2)]
        phase = shared[:].rearrange("p (b s) -> p b s", b=B)
        wst = shared[:].rearrange("p (w n) -> p w n", w=2)
        back = xnT[:].rearrange("p (r c) s -> p r c s", c=K)

        x_in = [sem(f"x_in{i}") for i in range(4)]
        consts_in, w_in, pads_out = sem("consts_in"), sem("w_in"), sem("pads_out")
        pool_const, dve_const = sem("pool_const"), sem("dve_const")
        pe_setup, dve_setup, act_setup = sem("pe_setup"), sem("dve_setup"), sem("act_setup")
        passed = sem("passed")
        stats_done, mv_done, var_done, rstd_done, xn_done = (sem(n) for n in (
            "stats_done", "mv_done", "var_done", "rstd_done", "xn_done"))
        turned, xnT2_done, xnT_done, logits_done = (sem(n) for n in (
            "turned", "xnT2_done", "xnT_done", "logits_done"))
        row_done, dx_done, skip_done = sem("row_done"), sem("dx_done"), sem("skip_done")
        gate, gate_max, gate_exp, gate_mask, ranked, p_ready, p_turned, pT_done, pos_ready, tile_ready = (
            sem(n) for n in ("gate", "gate_max", "gate_exp", "gate_mask", "ranked", "p_ready", "p_turned",
                             "pT_done", "pos_ready", "tile_ready"))
        dest_done, scattered = sem("dest_done"), [sem("scattered0"), sem("scattered1")]
        abs_done, absmax_done, scales_done, split = (sem(n) for n in (
            "abs_done", "absmax_done", "scales_done", "split"))
        w_scaled, w_high, w_low = sem("w_scaled"), sem("w_high"), sem("w_low")
        z_done, absz_done, relz_done, exp_done, ln_done, sum_done, t1, t2, phase_done = (sem(n) for n in (
            "z_done", "absz_done", "relz_done", "exp_done", "ln_done", "sum_done", "t1", "t2", "phase_done"))
        bc_done, sin_done, ab_done, cos_done, content_done, p1_done, p2_done, m1_done, m2_done, q1_done, q2_done, \
            qs_done, ret_done, out_done, acc_done, pTs_done = (sem(n) for n in (
                "bc_done", "sin_done", "ab_done", "cos_done", "content_done", "p1_done", "p2_done", "m1_done",
                "m2_done", "q1_done", "q2_done", "qs_done", "ret_done", "out_done", "acc_done", "pTs_done"))
        xs_in = [sem(f"xs_in{i}") for i in range(U)]
        xt_done, xh_done, xl_done, l1_done, gelu_done, hh_done, hl_done, l2_done, y_done = (sem(n) for n in (
            "xt_done", "xh_done", "xl_done", "l1_done", "gelu_done", "hh_done", "hl_done", "l2_done", "y_done"))
        y_out = [sem("y_out0"), sem("y_out1")]
        back_in = [sem(f"back_in{i}") for i in range(B // 2)]
        add0_done, add1_done, stored = sem("add0_done"), sem("add1_done"), sem("stored")

        block = ctx.enter_context(nc.Block())
        N_CONSTS = 15 + T // U
        LOADS = 4
        SPL = B // LOADS

        @block.sync
        def _(sp):
            for i in range(LOADS):
                sp.dma_start(acc[:, i * SPL * TPB:(i + 1) * SPL * TPB, :].rearrange("p (b j) d -> p b j d", j=TPB),
                             x_seq[:, i * SPL:(i + 1) * SPL]).then_inc(x_in[i], 16)
            sp.dma_start(wst[:, 0, :].rearrange("p (e f) -> p e f", e=E), W1.rearrange("e d f -> d e f")).then_inc(w_in, 16)
            sp.dma_start(wst[:, 1, :].rearrange("p (e c d) -> p e c d", e=E, c=CH),
                         W2.rearrange("e (c f) d -> f e c d", f=P)).then_inc(w_in, 16)

            sp.wait_ge(scattered[0], 16 * T)
            sp.wait_ge(scattered[1], 16 * T)
            sp.wait_ge(pads_out, 16)
            sp.wait_ge(ab_done, B)
            sp.wait_ge(sin_done, B)

            def load(k, q):
                need(sp, y_out[q % 2], 32 * (2 * k + q // 2 - 1))
                j = k * U + q
                sp.dma_start(xs[q], grouped[bass.ds(j * TILE, TILE), :].rearrange("(h p) c -> p h c", p=P)
                             ).then_inc(xs_in[q], 16)
            steps(sp, N_TILES, load)

            sp.wait_ge(y_out[0], 32 * ((N_TILES + 1) // 2))
            sp.wait_ge(y_out[1], 32 * (N_TILES // 2))
            sp.wait_ge(bc_done, B)
            sp.wait_ge(content_done, B)
            for b in range(B):
                if b >= B // 2:
                    sp.wait_ge(add1_done, b - B // 2 + 1)
                sp.dma_start(back[:, b % (B // 2)].rearrange("p c (j d) -> p c j d", j=TPB), eo_seq[:, :, b]
                             ).then_inc(back_in[b % (B // 2)], 16)
            for b in range(B):
                sp.wait_ge(add1_done, b + 1)
                sp.dma_start(out_seq[:, b], acc[:, b * TPB:(b + 1) * TPB, :]).then_inc(stored, 16)
            sp.wait_ge(stored, 16 * B)

        @block.gpsimd
        def _(pool):
            nc.gpsimd.memset(ident[:], 0.0)
            nc.gpsimd.memset(row0[:], 0.0)
            nc.gpsimd.memset(bout[:], 0.0)
            nc.gpsimd.memset(ones16[:], 1.0)
            nc.gpsimd.memset(zeros[:], 0.0)
            nc.gpsimd.memset(minus_half[:], -0.5)
            nc.gpsimd.memset(padrow[:], 0.0)
            nc.gpsimd.iota(desc[:], pattern=[[-1, E]], base=E, channel_multiplier=0,
                           allow_small_or_imprecise_dtypes=True)
            nc.gpsimd.iota(jrow[:], pattern=[[1, N_TILES]], base=0, channel_multiplier=0,
                           allow_small_or_imprecise_dtypes=True)
            nc.gpsimd.memset(b2diag[:], 0.0).then_inc(pool_const, 1)
            pool.wait_ge(pool_const, 1)
            nc.gpsimd.memset(row0[0:1, :], 1.0)
            nc.gpsimd.affine_select(out=ident[:], in_=ident[:], compare_op=ALU.not_equal, fill=1.0, base=0,
                                    pattern=[[-1, P]], channel_multiplier=1)
            nc.gpsimd.affine_select(out=before[:], in_=ones16[:], compare_op=ALU.is_gt, fill=0.0, base=0,
                                    pattern=[[1, P]], channel_multiplier=-1)
            nc.gpsimd.iota(padrow[:, D:ROW].bitcast(I32), pattern=[[0, 1]], base=NOWHERE,
                           channel_multiplier=0).then_inc(pool_const, 1)
            pool.wait_ge(pool_const, 2)

            def first(k, q):
                b, u = k * U + q, q % 2
                pool.wait_ge(mv_done, b + 1)
                pool.sem_inc(passed, 1)
                nc.gpsimd.tensor_scalar(vare[:, u, :], mv[:, u, :, 1], 1e-5, None, ALU.add).then_inc(var_done, 1)
                pool.wait_ge(var_done, b + 1)
                nc.gpsimd.tensor_tensor(rstd[:, u, :], vare[:, u, :], minus_half[:], ALU.pow).then_inc(rstd_done, 1)
                if isinstance(k, int) and k == 0 and q == 0:
                    pool.wait_ge(consts_in, 16 * N_CONSTS)
                pool.wait_ge(xn_done, TPB * (b + 1))
                nc.gpsimd.tensor_copy(row[:, bass.ds(b * TPB, TPB), 0:D], xn2[:, u]).then_inc(row_done, 1)
                nc.gpsimd.tensor_tensor(dx[:], xn2[:, u], dskip[:, None, :].to_broadcast([P, TPB, D]), ALU.mult
                                        ).then_inc(dx_done, 1)
                pool.wait_ge(dx_done, b + 1)
                nc.gpsimd.tensor_tensor(acc[:, bass.ds(b * TPB, TPB), :], acc[:, bass.ds(b * TPB, TPB), :], dx[:],
                                        ALU.add).then_inc(skip_done, 1)
                pool.wait_ge(skip_done, b + 1)
                pool.wait_ge(row_done, b + 1)
            steps(pool, B, first)

            for c in range(K):
                if c:
                    pool.wait_ge(scattered[0], 16 * T)
                nc.gpsimd.iota(row[:, :, D].bitcast(I32).rearrange("p (b j) -> p b j", j=TPB),
                               pattern=[[SEQ, B], [1, TPB]], base=c * TOK, channel_multiplier=TPB
                               ).then_inc(dest_done, 1)
                pool.wait_ge(dest_done, c + 1)
                if c == 0:
                    pool.wait_ge(pads_out, 16)
                    pool.wait_ge(pos_ready, 1)
                for t in range(T):
                    nc.gpsimd.indirect_dma_start(
                        grouped, bass.IndirectOffsetOnAxis(ap=pos[:, c, t:t + 1].bitcast(U32), axis=0),
                        row[:, t, :], None,
                        bounds_check=ROWS - 1, oob_is_err=False).then_inc(scattered[c], 16)
                if c == 0:
                    pool.wait_ge(abs_done, 2)
                    nc.gpsimd.partition_all_reduce(maxw[:], absw[:], P, RMAX).then_inc(absmax_done, 1)
                    for w, (hi, lo) in enumerate(((w1h, w1l), (w2h, w2l))):
                        pool.wait_ge(w_high, w + 1)
                        nc.gpsimd.tensor_tensor(lo[:], wst[:, w, :], hi[:], ALU.subtract).then_inc(w_low, 1)

            def scatter(k, q):
                j, u = k * U + q, q % 2
                pool.wait_ge(y_done, j + 1)
                pool.sem_inc(passed, 1)
                for h in range(HALF):
                    nc.gpsimd.indirect_dma_start(
                        expert_out, bass.IndirectOffsetOnAxis(ap=xs[q][:, h, D:ROW].bitcast(U32), axis=0),
                        ysb[u][:, h, :], None, bounds_check=K * TOK - 1, oob_is_err=False).then_inc(y_out[u], 16)
            steps(pool, N_TILES, scatter)

        @block.tensor
        def _(pe):
            pe.wait_ge(consts_in, 16 * N_CONSTS)
            pe.wait_ge(pool_const, 2)
            nc.tensor.transpose(ps[0:RANK, 0, 0:P], wdt1[:], ident[:])
            nc.tensor.transpose(ps[:, 1, 0:E * CH], b1rows[:], ident[0:E * CH, 0:E * CH]).then_inc(pe_setup, 1)
            pe.wait_ge(act_setup, 1)
            nc.tensor.matmul(ps[:, 2, 0:P], wdt1T[:], wdt2[:], start=True, stop=True)
            nc.tensor.matmul(ps[:, 3, 0:1], wdt2[:], cols[0:RANK, 2:3], start=True, stop=True).then_inc(pe_setup, 1)
            pe.wait_ge(act_setup, 4)

            def logits(k, q):
                b, u = k * U + q, q % 2
                pe.wait_ge(xnT2_done, b + 1)
                for j in range(TPB):
                    mm = nc.tensor.matmul(ps[:, 2, bass.ds((b * TPB + j) * E, E)], xnT2[:, u, j:SEQ:TPB], wG[:],
                                          start=True, stop=True, skip_group_check=True)
                mm.then_inc(logits_done, 1)

            def turn(k, q):
                b, u = k * U + q, q % 2
                need(pe, xnT_done, b - 1)
                pe.wait_ge(xn_done, TPB * (b + 1))
                for j in range(TPB):
                    mm = nc.tensor.transpose(ps[:, u, j * P:(j + 1) * P], xn2[:, u, j, :], ident[:])
                mm.then_inc(turned, 1)
                if isinstance(k, int) and k == 0 and q == 0:
                    return
                logits(*((k, q - 1) if q else (k - 1, U - 1)))
            steps(pe, B, turn)
            logits(B // U - 1, U - 1)

            pe.wait_ge(gate_mask, 1)
            nc.tensor.matmul(ps[:, 3, :], before[:], mask16[:].rearrange("p t e -> p (t e)"), start=True, stop=True)
            nc.tensor.matmul(ps[:, 4, :], ones16[:], mask16[:].rearrange("p t e -> p (t e)"), start=True, stop=True
                             ).then_inc(ranked, 1)
            pe.wait_ge(p_ready, 1)
            for g in range(U):
                mm = nc.tensor.transpose(ps[:, 5, g * P:(g + 1) * P],
                                         gw[:, g * 16:(g + 1) * 16, :].rearrange("p t e -> p (t e)"), ident[:])
            mm.then_inc(p_turned, 1)

            def z(k, q):
                b, u = k * U + q, q % 2
                need(pe, relz_done, b - 1)
                need(pe, absz_done, b - 1)
                nc.tensor.matmul(ps[:, u, :], wdt[:], xnT[:, bass.ds(b, 1), :].rearrange("p a s -> p (a s)"),
                                 start=True, stop=True).then_inc(z_done, 1)
            pe.wait_ge(xnT_done, B)
            steps(pe, B, z)

            pe.wait_ge(pos_ready, 1)

            def project(k, q):
                b, u = k * U + q, q % 2
                need(pe, acc_done, b - 1)
                if q == 0:
                    pe.wait_ge(pTs_done, k + 1)
                bank = ps[:, 6 + u, :]
                nc.tensor.matmul(bank, row0[:], bout[:, None, :].to_broadcast([P, TPB, D]),
                                 start=True, stop=False, skip_group_check=True)
                rows = slice(q * TPB * E, (q + 1) * TPB * E)
                nc.tensor.matmul(bank, pTs[rows, :], b2diag[rows].rearrange("p j d -> p (j d)"),
                                 start=False, stop=False, skip_group_check=True)
                pe.wait_ge(ret_done, b + 1)
                for j in range(TPB):
                    mm = nc.tensor.matmul(ps[:, 6 + u, j * D:(j + 1) * D], ret[:, u, j:SEQ:TPB], wO[:],
                                          start=False, stop=(j == TPB - 1), skip_group_check=True)
                mm.then_inc(out_done, 1)

            def write_read(k, q):
                b, u = k * U + q, q % 2
                need(pe, content_done, b - 1)
                need(pe, ret_done, b - 1)
                xb = xnT[:, bass.ds(b, 1), :].rearrange("p a s -> p (a s)")
                nc.tensor.matmul(ps[:, 2 + u, :], wB[:], xb, start=True, stop=True)
                nc.tensor.matmul(ps[:, 4 + u, :], wC[:], xb, start=True, stop=True).then_inc(bc_done, 1)
                if isinstance(k, int) and k == 0 and q == 0:
                    return
                project(*((k, q - 1) if q else (k - 1, U - 1)))
            steps(pe, B, write_read)
            project(B // U - 1, U - 1)

            pe.wait_ge(acc_done, B)
            pe.wait_ge(w_low, 2)
            pe.wait_ge(w_high, 2)
            pe.wait_ge(tile_ready, 1)

            def turn_tile(k, q):
                j, u = k * U + q, q % 2
                pe.wait_ge(xs_in[q], 16 * (k + 1))
                need(pe, xl_done, j - 1)
                for h in range(HALF):
                    mm = nc.tensor.transpose(ps[:, u, h * P:(h + 1) * P], xs[q][:, h, 0:D], ident[:])
                mm.then_inc(xt_done, 1)

            def expert_of(k, q):
                j = k * U + q
                return pe.value_load(tile_expert[0:1, bass.ds(j, 1)], min_val=0, max_val=E - 1)

            def layer1(k, q):
                j, u = k * U + q, q % 2
                e = expert_of(k, q)
                pe.wait_ge(xl_done, j + 1)
                need(pe, gelu_done, CH * (j - 1))
                for c in range(CH):
                    o = ps[:, 2 + 2 * u + c // 2, (c % 2) * TILE:(c % 2 + 1) * TILE]
                    hi, lo = (w[:, bass.ds(e * FF + c * P, P)] for w in (w1h, w1l))
                    nc.tensor.matmul(o, hi, xh[u], start=True, stop=False)
                    nc.tensor.matmul(o, hi, xl[u], start=False, stop=False)
                    nc.tensor.matmul(o, lo, xh[u], start=False, stop=True).then_inc(l1_done, 1)

            def layer2(k, q):
                j, u = k * U + q, q % 2
                e = expert_of(k, q)
                pe.wait_ge(hl_done, 2 * (j + 1))
                need(pe, y_done, j - 1)
                for h in range(HALF):
                    o = ps[:, 6 + u, h * D:(h + 1) * D]
                    for c in range(CH):
                        hi, lo = (w[:, bass.ds(e * FF + c * D, D)] for w in (w2h, w2l))
                        a, b = (v[u][:, c, h * P:(h + 1) * P] for v in (hh, hl))
                        nc.tensor.matmul(o, a, hi, start=(c == 0), stop=False, skip_group_check=True)
                        nc.tensor.matmul(o, a, lo, start=False, stop=False, skip_group_check=True)
                        mm = nc.tensor.matmul(o, b, hi, start=False, stop=(c == CH - 1), skip_group_check=True)
                mm.then_inc(l2_done, 1)

            def tile_step(k, q):
                layer1(k, q)
                if not (isinstance(k, int) and k * U + q + 1 >= N_TILES):
                    turn_tile(*((k, q + 1) if q + 1 < U else (k + 1, 0)))
                if not (isinstance(k, int) and k == 0 and q == 0):
                    layer2(*((k, q - 1) if q else (k - 1, U - 1)))
            turn_tile(0, 0)
            steps(pe, N_TILES, tile_step)
            layer2((N_TILES - 1) // U, (N_TILES - 1) % U)

        @block.scalar
        def _(act):
            def col(i, v, n=P):
                act.dma_start(cols[0:n, i:i + 1], v.rearrange("(a b) -> a b", b=1)).then_inc(consts_in, 16)
            for i, (v, n) in enumerate(((b_B, P), (b_C, P), (b_dt1, RANK), (b_dt2, P), (omega, P))):
                col(i, v, n)
            for dst, src in ((wB, W_B), (wC, W_C), (wO, W_out), (wG, Wg), (wdt1, W_dt1), (wdt2, W_dt2)):
                act.dma_start(dst[:], src).then_inc(consts_in, 16)
            act.dma_start(b1rows[:], b1.rearrange("e (c f) -> (e c) f", f=P)).then_inc(consts_in, 16)
            act.dma_start(dskip[:], D_skip.partition_broadcast(P)).then_inc(consts_in, 16)
            act.dma_start(bgate[:], bg.partition_broadcast(P)).then_inc(consts_in, 16)
            act.wait_ge(pool_const, 2)
            act.dma_start(bout[0:1, :], b_out.rearrange("(a d) -> a d", a=1)).then_inc(consts_in, 16)
            for t in range(T // U):
                act.dma_start(b2diag[t * E:(t + 1) * E, t % TPB, :], b2).then_inc(consts_in, 16)
            act.dma_start(grouped.rearrange("(p r) c -> p r c", p=P),
                          padrow[:, None, :].to_broadcast([P, ROWS // P, ROW])).then_inc(pads_out, 16)
            act.wait_ge(pe_setup, 1)
            nc.scalar.copy(wdt1T[:], ps[0:RANK, 0, 0:P]).then_inc(act_setup, 1)
            nc.scalar.copy(b1T[:], ps[:, 1, 0:E * CH]).then_inc(act_setup, 1)
            act.wait_ge(pe_setup, 2)
            nc.scalar.copy(wdt[:], ps[:, 2, 0:P]).then_inc(act_setup, 1)
            nc.scalar.activation(cols[:, 5:6], ps[:, 3, 0:1], ACT.Identity, bias=cols[:, 3:4]).then_inc(act_setup, 1)

            def keep(k, q):
                b, u = k * U + q, q % 2
                act.wait_ge(turned, b + 1)
                need(act, logits_done, b - 1)
                t = ps[:, u, :].rearrange("p (j n) -> p n j", j=TPB)
                nc.scalar.copy(xnT2[:, u, :].rearrange("p (n j) -> p n j", j=TPB), t).then_inc(xnT2_done, 1)
                nc.scalar.copy(xnT[:, bass.ds(b, 1), :].rearrange("p a (n j) -> p (a n) j", j=TPB), t
                               ).then_inc(xnT_done, 1)
            steps(act, B, keep)

            act.wait_ge(gate_max, 1)
            nc.scalar.activation(pr[:], lg[:], ACT.Exp).then_inc(gate_exp, 1)
            act.wait_ge(p_turned, 1)
            nc.scalar.copy(pT[:].rearrange("p g n -> p (g n)"), ps[:, 5, :]).then_inc(pT_done, 1)

            act.wait_ge(scales_done, 1)
            for w, hi in enumerate((w1h, w2h)):
                nc.scalar.activation(wst[:, w, :], wst[:, w, :], ACT.Copy, scale=scl[:, w:w + 1]).then_inc(w_scaled, 1)
                act.wait_ge(w_scaled, w + 1)
                nc.scalar.copy(hi[:], wst[:, w, :]).then_inc(w_high, 1)

            nc.scalar.preload_act_table(ACT.Ln)
            act.wait_ge(skip_done, B)
            act.wait_ge(pos_ready, 1)

            def softplus(k, q):
                b, u = k * U + q, q % 2
                act.wait_ge(z_done, b + 1)
                need(act, exp_done, b - 1)
                nc.scalar.activation(absz[:, u, :], ps[:, u, :], ACT.Abs, bias=cols[:, 5:6]).then_inc(absz_done, 1)
                act.wait_ge(absz_done, b + 1)
                need(act, ln_done, b - 1)
                nc.scalar.activation(ex[:, u, :], absz[:, u, :], ACT.Exp, scale=-1.0).then_inc(exp_done, 1)
                act.wait_ge(exp_done, b + 1)
                need(act, sum_done, b - 1)
                nc.scalar.activation(lnz[:, u, :], ex[:, u, :], ACT.Ln, bias=1.0).then_inc(ln_done, 1)
            steps(act, B, softplus)

            nc.scalar.preload_act_table(ACT.Sin)

            def waves(k, q):
                b, u = k * U + q, q % 2
                if q == 0:
                    act.wait_ge(pT_done, 1)
                    need(act, out_done, k * U)
                    nc.scalar.copy(pTs[:], pT[:, bass.ds(k, 1), :].rearrange("p a n -> p (a n)")).then_inc(pTs_done, 1)
                act.wait_ge(phase_done, b + 1)
                need(act, q2_done, b - 1)
                need(act, q1_done, b - 1)
                f = phase[:, bass.ds(b, 1), :].rearrange("p a s -> p (a s)")
                nc.scalar.activation(sn[:, u, :], f, ACT.Sin, scale=TWO_PI).then_inc(sin_done, 1)
                nc.scalar.activation(ab[:, u, :], f, ACT.Abs).then_inc(ab_done, 1)
                act.wait_ge(ab_done, b + 1)
                nc.scalar.activation(cs[:, u, :], ab[:, u, :], ACT.Sin, scale=-TWO_PI, bias=cols[:, 7:8]
                                     ).then_inc(cos_done, 1)
            act.wait_ge(phase_done, B)
            act.wait_ge(ln_done, B)
            steps(act, B, waves)

            nc.scalar.preload_act_table(ACT.Gelu)
            act.wait_ge(ab_done, B)
            act.wait_ge(cos_done, B)

            def high(k, q):
                j, u = k * U + q, q % 2
                act.wait_ge(xt_done, j + 1)
                need(act, l1_done, CH * (j - 1))
                nc.scalar.copy(xh[u], ps[:, u, 0:TILE]).then_inc(xh_done, 1)

            def gelu(k, q):
                j, u = k * U + q, q % 2
                e = act.value_load(tile_expert[0:1, bass.ds(j, 1)], min_val=0, max_val=E - 1)
                need(act, hl_done, 2 * (j - 1))
                for c in range(CH):
                    act.wait_ge(l1_done, CH * j + 2 * (c // 2) + 2)
                    nc.scalar.activation(gel[u][:, c, :], ps[:, 2 + 2 * u + c // 2, (c % 2) * TILE:(c % 2 + 1) * TILE],
                                         ACT.Gelu, bias=b1T[:, bass.ds(e * CH + c, 1)], scale=scl[:, 2:3]
                                         ).then_inc(gelu_done, 1)

            def result(k, q):
                j, u = k * U + q, q % 2
                act.wait_ge(l2_done, j + 1)
                need(act, y_out[u], 32 * (2 * k + q // 2))
                nc.scalar.activation(ysb[u].rearrange("p h d -> p (h d)"), ps[:, 6 + u, 0:HALF * D], ACT.Copy,
                                     scale=scl[:, 4:5]).then_inc(y_done, 1)

            def tile_step(k, q):
                gelu(k, q)
                if not (isinstance(k, int) and k * U + q + 1 >= N_TILES):
                    high(*((k, q + 1) if q + 1 < U else (k + 1, 0)))
                if not (isinstance(k, int) and k == 0 and q == 0):
                    result(*((k, q - 1) if q else (k - 1, U - 1)))
            act.wait_ge(tile_ready, 1)
            high(0, 0)
            steps(act, N_TILES, tile_step)
            result((N_TILES - 1) // U, (N_TILES - 1) % U)

        @block.vector
        def _(dve):
            def norm(k, q):
                b, u = k * U + q, q % 2
                need(dve, row_done, b - 1)
                need(dve, dx_done, b - 1)
                need(dve, turned, b - 1)
                dve.wait_ge(rstd_done, b + 1)
                for j in range(TPB):
                    nc.vector.tensor_scalar(xn2[:, u, j, :], acc[:, bass.ds(b * TPB + j, 1), :].rearrange(
                        "p a d -> p (a d)"), mv[:, u, j, 0:1], rstd[:, u, j:j + 1], ALU.subtract, ALU.mult
                                            ).then_inc(xn_done, 1)

            def moments(k, q):
                b, u = k * U + q, q % 2
                if isinstance(k, int) and q == 0:
                    dve.wait_ge(x_in[0], 16)
                need(dve, xn_done, TPB * (b - 1))
                for j in range(TPB):
                    mm = nc.vector.bn_stats(stats[:, u, j, :], acc[:, bass.ds(b * TPB + j, 1), :].rearrange(
                        "p a d -> p (a d)"))
                mm.then_inc(stats_done, 1)
                dve.wait_ge(stats_done, b + 1)
                dve.sem_inc(passed, 1)
                for j in range(TPB):
                    mm = nc.vector.bn_aggr(mv[:, u, j, :], stats[:, u, j, :])
                mm.then_inc(mv_done, 1)
                if isinstance(k, int) and k == 0 and q == 0:
                    for i in range(1, LOADS):
                        dve.wait_ge(x_in[i], 16)
                    return
                norm(*((k, q - 1) if q else (k - 1, U - 1)))
            steps(dve, B, moments)
            norm(B // U - 1, U - 1)

            n_gate = [0]

            def link(ins):
                n_gate[0] += 1
                ins.then_inc(gate, 1)
                dve.wait_ge(gate, n_gate[0])

            def over_e(v):
                return v[:, :, None].to_broadcast([P, T, E])

            V = nc.vector
            dve.wait_ge(logits_done, B)
            dve.wait_ge(pool_const, 2)
            dve.wait_ge(consts_in, 16 * N_CONSTS)
            link(V.memset(cols[:, 7:8], 1.5707963))
            link(V.tensor_scalar(cols[:, 6:7], cols[:, 4:5], 1.0 / 6.283185307179586, None, ALU.mult))
            link(V.tensor_tensor(lg[:], ps[:, 2, :].rearrange("p (t e) -> p t e", e=E),
                                 bgate[:, None, :].to_broadcast([P, T, E]), ALU.add))
            link(V.tensor_reduce(mx[:], lg[:], AX, ALU.max))
            V.tensor_tensor(lg[:], lg[:], over_e(mx[:]), ALU.subtract).then_inc(gate_max, 1)
            dve.wait_ge(gate_exp, 1)
            link(V.tensor_reduce(sm[:], pr[:], AX, ALU.add))
            link(V.reciprocal(sm[:], sm[:]))
            link(V.tensor_tensor(pr[:], pr[:], over_e(sm[:]), ALU.mult))
            rest = pr
            for c, one_hot in ((0, g1), (1, g2)):
                link(V.tensor_reduce(m12[:, c, :], rest[:], AX, ALU.max))
                link(V.tensor_tensor(one_hot[:], rest[:], over_e(m12[:, c, :]), ALU.is_equal))
                link(V.tensor_tensor(one_hot[:], one_hot[:], desc[:, None, :].to_broadcast([P, T, E]), ALU.mult))
                link(V.tensor_reduce(mx[:], one_hot[:], AX, ALU.max))
                link(V.tensor_tensor(one_hot[:], one_hot[:], over_e(mx[:]), ALU.is_equal))
                if c == 0:
                    rest = lg
                    link(V.scalar_tensor_tensor(out=lg[:].rearrange("p t e -> p (t e)"),
                                                in0=g1[:].rearrange("p t e -> p (t e)"), scalar=-2.0,
                                                in1=pr[:].rearrange("p t e -> p (t e)"), op0=ALU.mult, op1=ALU.add))
            V.tensor_tensor(mask16[:], g1[:], g2[:], ALU.add).then_inc(gate_mask, 1)
            dve.wait_ge(gate_mask, 1)
            link(V.tensor_tensor(den[:], m12[:, 0, :], m12[:, 1, :], ALU.add))
            link(V.tensor_scalar(den0[:], den[:], 0.0, None, ALU.is_equal))
            link(V.tensor_tensor(den[:], den[:], den0[:], ALU.add))
            link(V.reciprocal(den[:], den[:]))
            link(V.tensor_tensor(gk[:, 0, :], m12[:, 0, :], den[:], ALU.mult))
            link(V.tensor_tensor(gk[:, 1, :], m12[:, 1, :], den[:], ALU.mult))
            link(V.tensor_tensor(pr[:], pr[:], mask16[:], ALU.mult))
            V.tensor_tensor(gw[:], pr[:], over_e(den[:]), ALU.mult).then_inc(p_ready, 1)
            dve.wait_ge(p_ready, 1)

            dve.wait_ge(ranked, 1)
            dve.wait_ge(row_done, B)
            dve.wait_ge(dx_done, B)
            link(V.tensor_copy(tot, ps[:, 4, :].rearrange("p (t e) -> p e t", e=E)))
            for e in range(E):
                i = V.tensor_tensor_scan(cum[:, e, :], tot[:, e, :], zeros[:, 0:T], 0.0, ALU.add, ALU.add)
            link(i)
            count, tiles, ends, start = (sizes[:, i, :] for i in range(4))
            link(V.tensor_copy(count, cum[:, :, T - 1]))
            link(V.tensor_scalar(tiles, count, 1.0 / TILE, (TILE - 1.0) / TILE - 0.5 + 0.5 / TILE, ALU.mult, ALU.add))
            link(V.tensor_scalar(tiles, tiles, ROUND, None, ALU.add))
            link(V.tensor_scalar(tiles, tiles, ROUND, None, ALU.subtract))
            link(V.tensor_tensor_scan(ends, tiles, zeros[:, 0:E], 0.0, ALU.add, ALU.add))
            link(V.tensor_tensor(start, ends, tiles, ALU.subtract))
            link(V.tensor_scalar(start, start, float(TILE), None, ALU.mult))
            link(V.tensor_tensor(cum, cum, tot, ALU.subtract))
            link(V.tensor_tensor(cum, cum, start[:, :, None].to_broadcast([P, E, T]), ALU.add))
            link(V.tensor_tensor(lg[:], ps[:, 3, :].rearrange("p (t e) -> p t e", e=E),
                                 cum.rearrange("p e t -> p t e"), ALU.add))
            for c, one_hot in ((0, g1), (1, g2)):
                link(V.tensor_tensor(one_hot[:], one_hot[:], lg[:], ALU.mult))
                link(V.tensor_reduce(posf[:, c, :], one_hot[:], AX, ALU.add))
            V.tensor_copy(pos[:], posf[:]).then_inc(pos_ready, 1)
            link(V.tensor_tensor(past, jrow[:, :, None].to_broadcast([P, N_TILES, E]),
                                 ends[:, None, :].to_broadcast([P, N_TILES, E]), ALU.is_ge))
            link(V.tensor_reduce(tile_e[:], past, AX, ALU.add))
            V.tensor_scalar(tile_expert[:], tile_e[:], float(E - 1), None, ALU.min).then_inc(tile_ready, 1)

            dve.wait_ge(w_in, 32)
            for w in range(2):
                V.tensor_reduce(absw[:, w:w + 1], wst[:, w, :], AX, ALU.max, apply_absolute_value=True
                                ).then_inc(abs_done, 1)
            dve.wait_ge(absmax_done, 1)
            link(V.tensor_scalar(pw[:].bitcast(I32), maxw[:].bitcast(I32), 0x7F800000, None, ALU.bitwise_and))
            link(V.tensor_scalar(pw[:], pw[:], 2.0 ** -60, 2.0 ** 60, ALU.max, ALU.min))
            link(V.reciprocal(scl[:, 6:8], pw[:]))
            link(V.tensor_scalar(scl[:, 0:2], scl[:, 6:8], 2.0 ** 12, None, ALU.mult))
            link(V.tensor_scalar(scl[:, 2:3], pw[:, 0:1], 2.0 ** -12, None, ALU.mult))
            V.tensor_scalar(scl[:, 4:5], pw[:, 1:2], 2.0 ** -12, None, ALU.mult).then_inc(scales_done, 1)

            bdt, w_turn = cols[:, 5:6], cols[:, 6:7]

            def accumulate(k, q):
                b, u = k * U + q, q % 2
                dve.wait_ge(ln_done, b + 1)
                dve.wait_ge(relz_done, b + 1)
                need(dve, phase_done, b)
                V.tensor_tensor_scan(steps_sum, relz[:, u, :], lnz[:, u, :], 0.0, ALU.add, ALU.add
                                     ).then_inc(sum_done, 1)
                dve.wait_ge(sum_done, b + 1)
                V.tensor_scalar(turns, steps_sum, w_turn, ROUND, ALU.mult, ALU.add).then_inc(t1, 1)
                dve.wait_ge(t1, b + 1)
                V.tensor_scalar(whole, turns, ROUND, None, ALU.subtract).then_inc(t2, 1)
                dve.wait_ge(t2, b + 1)
                V.scalar_tensor_tensor(out=phase[:, bass.ds(b, 1), :].rearrange("p a s -> p (a s)"),
                                       in0=steps_sum, scalar=w_turn, in1=whole, op0=ALU.mult, op1=ALU.subtract
                                       ).then_inc(phase_done, 1)

            def magnitudes(k, q):
                b, u = k * U + q, q % 2
                dve.wait_ge(absz_done, b + 1)
                need(dve, sum_done, b - 1)
                V.tensor_scalar(relz[:, u, :], ps[:, u, :], bdt, 0.0, ALU.add, ALU.max).then_inc(relz_done, 1)
                if isinstance(k, int) and k == 0 and q == 0:
                    return
                accumulate(*((k, q - 1) if q else (k - 1, U - 1)))
            dve.wait_ge(act_setup, 4)
            dve.wait_ge(p_turned, 1)
            dve.wait_ge(skip_done, B)
            dve.wait_ge(w_low, 2)
            steps(dve, B, magnitudes)
            accumulate(B // U - 1, U - 1)

            def add_out(k, q):
                b, u = k * U + q, q % 2
                dve.wait_ge(out_done, b + 1)
                a = acc[:, bass.ds(b * TPB, TPB), :].rearrange("p j d -> p (j d)")
                V.tensor_tensor(a, ps[:, 6 + u, :], a, ALU.add).then_inc(acc_done, 1)

            def recall(k, q):
                b, u = k * U + q, q % 2
                xb = xnT[:, bass.ds(b, 1), :].rearrange("p a s -> p (a s)")
                dve.wait_ge(bc_done, b + 1)
                need(dve, ret_done, b)
                V.scalar_tensor_tensor(out=content, in0=ps[:, 2 + u, :], scalar=cols[:, 0:1], in1=xb,
                                       op0=ALU.add, op1=ALU.mult).then_inc(content_done, 1)
                dve.wait_ge(content_done, b + 1)
                dve.wait_ge(cos_done, b + 1)
                V.tensor_tensor(p1, content, cs[:, u, :], ALU.mult).then_inc(p1_done, 1)
                V.tensor_tensor(p2, content, sn[:, u, :], ALU.mult).then_inc(p2_done, 1)
                dve.wait_ge(p1_done, b + 1)
                V.tensor_tensor_scan(m1, p1, zeros[:], 0.0, ALU.add, ALU.add).then_inc(m1_done, 1)
                dve.wait_ge(p2_done, b + 1)
                V.tensor_tensor_scan(m2[:], p2, zeros[:], 0.0, ALU.add, ALU.add).then_inc(m2_done, 1)
                dve.wait_ge(m1_done, b + 1)
                V.tensor_tensor(q1, m1, cs[:, u, :], ALU.mult).then_inc(q1_done, 1)
                dve.wait_ge(m2_done, b + 1)
                V.tensor_tensor(q2, m2[:], sn[:, u, :], ALU.mult).then_inc(q2_done, 1)
                dve.wait_ge(q2_done, b + 1)
                dve.wait_ge(q1_done, b + 1)
                V.tensor_tensor(qs, q1, q2, ALU.add).then_inc(qs_done, 1)
                dve.wait_ge(qs_done, b + 1)
                need(dve, out_done, b - 1)
                V.scalar_tensor_tensor(out=ret[:, u, :], in0=ps[:, 4 + u, :], scalar=cols[:, 1:2], in1=qs,
                                       op0=ALU.add, op1=ALU.mult).then_inc(ret_done, 1)
                if isinstance(k, int) and k == 0 and q == 0:
                    return
                add_out(*((k, q - 1) if q else (k - 1, U - 1)))
            dve.wait_ge(phase_done, B)
            steps(dve, B, recall)
            add_out(B // U - 1, U - 1)

            def low(k, q):
                j, u = k * U + q, q % 2
                dve.wait_ge(xh_done, j + 1)
                need(dve, l1_done, CH * (j - 1))
                V.tensor_tensor(xl[u], ps[:, u, 0:TILE], xh[u], ALU.subtract).then_inc(xl_done, 1)

            def hidden(k, q):
                j, u = k * U + q, q % 2
                need(dve, l2_done, j - 1)
                for i in range(2):
                    dve.wait_ge(gelu_done, CH * j + 2 * i + 2)
                    g, a, b = (v[u][:, 2 * i:2 * i + 2, :].rearrange("p c n -> p (c n)") for v in (gel, hh, hl))
                    V.tensor_scalar(a, g, H_SCALE, None, ALU.mult).then_inc(hh_done, 1)
                    dve.wait_ge(hh_done, 2 * j + i + 1)
                    V.scalar_tensor_tensor(out=b, in0=g, scalar=H_SCALE, in1=a, op0=ALU.mult, op1=ALU.subtract
                                           ).then_inc(hl_done, 1)

            def tile_step(k, q):
                hidden(k, q)
                if not (isinstance(k, int) and k * U + q + 1 >= N_TILES):
                    low(*((k, q + 1) if q + 1 < U else (k + 1, 0)))
            low(0, 0)
            steps(dve, N_TILES, tile_step)

            dve.wait_ge(acc_done, B)
            for b in range(B):
                r = b % (B // 2)
                dve.wait_ge(back_in[r], 16 * (b // (B // 2) + 1))
                for c in range(K):
                    if c:
                        dve.wait_ge(add0_done, b + 1)
                    for j in range(TPB):
                        t = b * TPB + j
                        i = V.scalar_tensor_tensor(out=acc[:, t, :], in0=back[:, r, c, j * D:(j + 1) * D],
                                                   scalar=gk[:, c, t:t + 1], in1=acc[:, t, :],
                                                   op0=ALU.mult, op1=ALU.add)
                    i.then_inc((add0_done, add1_done)[c], 1)


H_SCALE = 1.0


_INS = ["x", "W_B", "b_B", "W_C", "b_C", "W_dt1", "b_dt1", "W_dt2", "b_dt2", "omega_base", "D", "W_out", "b_out"]
_FFN = ["W1", "b1", "W2", "b2", "Wg", "bg"]


def kernel(**inputs):
    import numpy as np
    import concourse.bacc as bacc
    from concourse import mybir as _mybir
    from concourse.bass_utils import run_bass_kernel_spmd

    nc = bacc.Bacc("TRN2", target_bir_lowering=False, num_devices=1)
    arrays, args = {}, []
    for name in ["L0_attn_" + n for n in _INS] + ["L0_ffn_" + n for n in _FFN]:
        a = np.ascontiguousarray(inputs[name])
        if name == "L0_attn_x":
            a = a.reshape(TOK, D)
        arrays["in_" + name] = a
        args.append(nc.dram_tensor("in_" + name, a.shape, _mybir.dt.from_np(a.dtype), kind="ExternalInput").ap())
    out = nc.dram_tensor("out_0", (TOK, D), F32, kind="ExternalOutput").ap()
    program(nc, *args, out)
    r = run_bass_kernel_spmd(nc, [arrays], core_ids=[0])
    return r.results[0]["out_0"].reshape(B, SEQ, D)
```

```python
from contextlib import ExitStack

import concourse.bass as bass
from concourse import mybir

ALU = mybir.AluOpType
ACT = mybir.ActivationFunctionType
F32 = mybir.dt.float32
F16 = mybir.dt.float16
BF16 = mybir.dt.bfloat16
I32 = mybir.dt.int32
U32 = mybir.dt.uint32
AX = mybir.AxisListType.X
RMAX = bass.bass_isa.ReduceOp.max

P = 128
B, SEQ, D = 16, 512, 128
TOK = B * SEQ
TPB = SEQ // P
T = B * TPB
E, FF, K = 8, 512, 2
CH = FF // P
RANK = 32
TILE = 256
HALF = TILE // P
N_TILES = K * TOK // TILE + E - 1
ROWS = N_TILES * TILE
ROW = D + 1
NOWHERE = 65535
ROUND = 1.5 * 2.0 ** 23
TWO_PI = 6.283185
U = 4
FU = 8


def need(eng, sem, count):
    if isinstance(count, int) and count <= 0:
        return
    eng.wait_ge(sem, count)


def steps(eng, n, body, unroll=U, peel=1, between=None, done=0):
    for j in range(done, peel * unroll):
        body(j // unroll, j % unroll)
    if between:
        between()
    with eng.Fori(peel, n // unroll) as k:
        for q in range(unroll):
            body(k, q)
    for j in range(n // unroll * unroll, n):
        body(j // unroll, j % unroll)


def program(nc, x, W_B, b_B, W_C, b_C, W_dt1, b_dt1, W_dt2, b_dt2, omega, D_skip, W_out, b_out,
            W1, b1, W2, b2, Wg, bg, out):
    with ExitStack() as ctx:
        def sb(name, shape, dt=F32):
            return ctx.enter_context(nc.sbuf_tensor(name, shape, dt))

        def sem(name):
            return ctx.enter_context(nc.semaphore(name))

        grouped = nc.dram_tensor("grouped", (ROWS, ROW), F32, kind="Internal").ap()
        expert_out = nc.dram_tensor("expert_out", (K * TOK, D), F32, kind="Internal").ap()

        x_seq = x.rearrange("(b p j) d -> p b j d", p=P, j=TPB)
        out_seq = out.rearrange("(b p j) d -> p b j d", p=P, j=TPB)
        eo_seq = expert_out.rearrange("(c b p j) d -> p c b j d", p=P, j=TPB, c=K)

        ps = ctx.enter_context(nc.psum_tensor("ps", [P, 8, 512], F32))

        acc = sb("acc", [P, T, D])
        row = sb("row", [P, T, ROW])
        xnT = sb("xnT", [P, B, SEQ])
        shared = sb("shared", [P, B * SEQ])
        w1 = sb("w1", [P, 2 * E * FF], F16)
        w1h, w1l = w1[:, 0:E * FF], w1[:, E * FF:]
        w2h = sb("w2h", [P, E * FF], F16)
        w2l = sb("w2l", [P, E * FF], F16)
        ident = sb("ident", [P, P])
        before = sb("before", [P, P], BF16)
        ones16 = sb("ones16", [P, P], BF16)
        wB = sb("wB", [P, D])
        wC = sb("wC", [P, D])
        wO = sb("wO", [P, D])
        wG = sb("wG", [P, E])
        wdt1 = sb("wdt1", [P, RANK])
        wdt1T = sb("wdt1T", [RANK, P])
        wdt2 = sb("wdt2", [RANK, P])
        wdt = sb("wdt", [P, P])
        cols = sb("cols", [P, 8])
        bout = sb("bout", [P, D])
        skip = sb("skip", [P, D])
        bgate = sb("bgate", [P, E])
        b1rows = sb("b1rows", [E * CH, P])
        b1T = sb("b1T", [P, E * CH])
        b2diag = sb("b2diag", [P, TPB, D])
        pT = sb("pT", [P, U, P])
        pTs = sb("pTs", [P, P])
        padrow = sb("padrow", [P, ROW])
        maxsq = sb("maxsq", [P, 2])
        pw = sb("pw", [P, 4])
        b1m = sb("b1m", [P, 1])
        b1max = sb("b1max", [P, 1])
        scl = sb("scl", [P, 8])
        xn2 = sb("xn2", [P, 2, TPB, D])
        xnT2 = sb("xnT2", [P, 2, SEQ])
        mean = sb("mean", [P, T])
        vare = sb("vare", [P, T])
        gap = sb("gap", [P, T])
        rstd = sb("rstd", [P, T])
        pwi = pw[:, 0:2].bitcast(I32)
        minus_half = sb("minus_half", [P, U * TPB])
        accumulated = sb("accumulated", [P, SEQ])
        goes = sb("goes", [P, U, HALF], I32)
        lg = sb("lg", [P, T, E])
        pr = sb("pr", [P, T, E])
        gw = sb("gw", [P, T, E])
        g1 = sb("g1", [P, T, E])
        g2 = sb("g2", [P, T, E])
        stats = g2[:].rearrange("p t e -> p (t e)")[:, 0:T * 6].rearrange("p (t c) -> p t c", c=6)
        mask16 = sb("mask16", [P, T, E], BF16)
        mx = sb("mx", [P, T])
        sm = sb("sm", [P, T])
        m12 = sb("m12", [P, K, T])
        gk = sb("gk", [P, K, T])
        den = sb("den", [P, T])
        den0 = sb("den0", [P, T])
        pos = sb("pos", [P, K, T], I32)
        posf = sb("posf", [P, K, T])
        desc = sb("desc", [P, E])
        jrow = sb("jrow", [P, N_TILES])
        skipped = [v[:].rearrange("p t e -> p (t e)").rearrange("p (j d) -> p j d", j=TPB) for v in (lg, pr, gw, g1)]
        tot, cum = (xn2[:, u].rearrange("p j d -> p (j d)").rearrange("p (e t) -> p e t", e=E) for u in range(2))
        zeros = sb("zeros", [P, SEQ])
        sizes = sb("sizes", [P, 8, E])
        past = xnT2[:].rearrange("p u s -> p (u s)")[:, 0:N_TILES * E].rearrange("p (n e) -> p n e", e=E)
        tile_e = sb("tile_e", [P, N_TILES])
        tile_expert = sb("tile_expert", [P, N_TILES], I32)
        tile_column = sb("tile_column", [P, N_TILES], I32)
        def flat(v):
            return v[:].rearrange("p a b -> p (a b)")

        absz, relz = xn2[:].rearrange("p u j d -> p u (j d)"), xnT2
        ex = sb("ex", [P, 2, SEQ])
        lnz = sb("lnz", [P, 2, SEQ])
        ret = lnz
        steps_sum = accumulated[:]
        turns, whole = flat(pr), flat(gw)
        sn, ab, cs = absz, relz, ex
        content, p1, m1 = flat(g1), flat(g2), flat(lg)
        p2, m2 = turns, steps_sum
        q1, q2, qs = m1, m2, content

        at = [0]

        def cut(n, dt=F32):
            words = n * (2 if dt == F16 else 4) // 4
            v = shared[:, at[0]:at[0] + words]
            at[0] += words
            return v.bitcast(dt) if dt != F32 else v

        xs = [cut(HALF * ROW).rearrange("p (h c) -> p h c", h=HALF) for _ in range(U)]
        xh = [cut(TILE, F16) for _ in range(U)]
        xl = [cut(TILE, F16) for _ in range(U)]
        gel = [cut(CH * TILE).rearrange("p (c n) -> p c n", c=CH) for _ in range(2)]
        hh = [cut(CH * TILE, F16).rearrange("p (c n) -> p c n", c=CH) for _ in range(2)]
        hl = [cut(CH * TILE, F16).rearrange("p (c n) -> p c n", c=CH) for _ in range(2)]
        ysb = [cut(HALF * D).rearrange("p (h d) -> p h d", h=HALF) for _ in range(2)]
        phase = shared[:].rearrange("p (b s) -> p b s", b=B)
        squares = w1[:].rearrange("p (b n) -> p b n", b=B)
        sumsq, topsq = den[:, 0:B], den0[:, 0:2]
        wst = shared[:].rearrange("p (w n) -> p w n", w=2)
        back = xnT[:].rearrange("p (r c) s -> p r c s", c=K)

        x_in = [sem(f"x_in{i}") for i in range(4)]
        consts_in, w_in, b2_in, pads_out = sem("consts_in"), sem("w_in"), sem("b2_in"), sem("pads_out")
        pool_const, dve_const = sem("pool_const"), sem("dve_const")
        pe_setup, dve_setup, act_setup = sem("pe_setup"), sem("dve_setup"), sem("act_setup")
        passed = sem("passed")
        stats_done, moment, var_done, rstd_done, xn_done = (sem(n) for n in (
            "stats_done", "moment", "var_done", "rstd_done", "xn_done"))
        turned, xnT2_done, xnT_done, logits_done = (sem(n) for n in (
            "turned", "xnT2_done", "xnT_done", "logits_done"))
        row_done, skip_done, bout_done, bias_done = (sem(n) for n in (
            "row_done", "skip_done", "bout_done", "bias_done"))
        gate, gate_max, gate_exp, gate_mask, ranked, p_ready, p_turned, pT_done, pos_ready, tile_ready = (
            sem(n) for n in ("gate", "gate_max", "gate_exp", "gate_mask", "ranked", "p_ready", "p_turned",
                             "pT_done", "pos_ready", "tile_ready"))
        dest_done, scattered = sem("dest_done"), [sem("scattered0"), sem("scattered1")]
        topsq_done = sem("topsq_done")
        sumsq_done, maxsq_done, scales_done, scale_step, b1max_done = (sem(n) for n in (
            "sumsq_done", "maxsq_done", "scales_done", "scale_step", "b1max_done"))
        w_scaled, w_high, w_low = sem("w_scaled"), sem("w_high"), sem("w_low")
        z_done, absz_done, relz_done, exp_done, ln_done, sum_done, t1, t2, phase_done = (sem(n) for n in (
            "z_done", "absz_done", "relz_done", "exp_done", "ln_done", "sum_done", "t1", "t2", "phase_done"))
        bc_done, sin_done, ab_done, cos_done, content_done, p1_done, p2_done, m1_done, m2_done, q1_done, q2_done, \
            qs_done, ret_done, out_done, acc_done, pTs_done = (sem(n) for n in (
                "bc_done", "sin_done", "ab_done", "cos_done", "content_done", "p1_done", "p2_done", "m1_done",
                "m2_done", "q1_done", "q2_done", "qs_done", "ret_done", "out_done", "acc_done", "pTs_done"))
        xs_in = [sem(f"xs_in{i}") for i in range(U)]
        xt_done, xh_done, xl_done, l1_done, gelu_done, hh_done, hl_done, l2_done, y_done = (sem(n) for n in (
            "xt_done", "xh_done", "xl_done", "l1_done", "gelu_done", "hh_done", "hl_done", "l2_done", "y_done"))
        y_out = [sem("y_out0"), sem("y_out1")]
        goes_done = sem("goes_done")
        back_in = [sem(f"back_in{i}") for i in range(B // 2)]
        add0_done, add1_done, stored = sem("add0_done"), sem("add1_done"), sem("stored")

        block = ctx.enter_context(nc.Block())
        N_CONSTS = 15
        LOADS = 4
        SPL = B // LOADS

        @block.sync
        def _(sp):
            def load_x(i):
                sp.dma_start(acc[:, i * SPL * TPB:(i + 1) * SPL * TPB, :].rearrange("p (b j) d -> p b j d", j=TPB),
                             x_seq[:, i * SPL:(i + 1) * SPL]).then_inc(x_in[i], 16)
            load_x(0)
            load_x(1)
            sp.wait_ge(x_in[0], 16)
            load_x(2)
            load_x(3)
            sp.wait_ge(consts_in, 16 * N_CONSTS)
            sp.dma_start(wst[:, 0, :].rearrange("p (e f) -> p e f", e=E), W1.rearrange("e d f -> d e f")).then_inc(w_in, 16)
            sp.dma_start(wst[:, 1, :].rearrange("p (e c d) -> p e c d", e=E, c=CH),
                         W2.rearrange("e (c f) d -> f e c d", f=P)).then_inc(w_in, 16)
            sp.wait_ge(pool_const, 2)
            for t in range(T // U):
                sp.dma_start(b2diag[t * E:(t + 1) * E, t % TPB, :], b2).then_inc(b2_in, 16)
            sp.dma_start(grouped.rearrange("(p r) c -> p r c", p=P),
                         padrow[:, None, :].to_broadcast([P, ROWS // P, ROW])).then_inc(pads_out, 16)

            sp.wait_ge(scattered[0], 16 * T)
            sp.wait_ge(scattered[1], 16 * T)
            sp.wait_ge(pads_out, 16)
            sp.wait_ge(ab_done, B)
            sp.wait_ge(sin_done, B)

            def load(k, q):
                j = k * U + q
                need(sp, goes_done, j - U + 1)
                need(sp, xt_done, j - U + 1)
                sp.dma_start(xs[q], grouped[bass.ds(j * TILE, TILE), :].rearrange("(h p) c -> p h c", p=P)
                             ).then_inc(xs_in[q], 16)
            steps(sp, N_TILES, load)

            sp.wait_ge(y_out[0], 32 * ((N_TILES + 1) // 2))
            sp.wait_ge(y_out[1], 32 * (N_TILES // 2))
            sp.wait_ge(bc_done, B)
            sp.wait_ge(content_done, B)
            for b in range(B):
                if b >= B // 2:
                    sp.wait_ge(add1_done, b - B // 2 + 1)
                sp.dma_start(back[:, b % (B // 2)].rearrange("p c (j d) -> p c j d", j=TPB), eo_seq[:, :, b]
                             ).then_inc(back_in[b % (B // 2)], 16)

        @block.gpsimd
        def _(pool):
            nc.gpsimd.memset(ident[:], 0.0)
            nc.gpsimd.memset(ones16[:], 1.0)
            nc.gpsimd.memset(zeros[:], 0.0)
            nc.gpsimd.memset(minus_half[:], -0.5)
            nc.gpsimd.memset(padrow[:], 0.0)
            nc.gpsimd.iota(desc[:], pattern=[[-1, E]], base=E, channel_multiplier=0,
                           allow_small_or_imprecise_dtypes=True)
            nc.gpsimd.iota(jrow[:], pattern=[[1, N_TILES]], base=0, channel_multiplier=0,
                           allow_small_or_imprecise_dtypes=True)
            nc.gpsimd.memset(b2diag[:], 0.0).then_inc(pool_const, 1)
            pool.wait_ge(pool_const, 1)
            nc.gpsimd.affine_select(out=ident[:], in_=ident[:], compare_op=ALU.not_equal, fill=1.0, base=0,
                                    pattern=[[-1, P]], channel_multiplier=1)
            nc.gpsimd.affine_select(out=before[:], in_=ones16[:], compare_op=ALU.is_gt, fill=0.0, base=0,
                                    pattern=[[1, P]], channel_multiplier=-1)
            nc.gpsimd.iota(padrow[:, D:ROW].bitcast(I32), pattern=[[0, 1]], base=NOWHERE,
                           channel_multiplier=0).then_inc(pool_const, 1)
            pool.wait_ge(pool_const, 2)

            def first(k, q):
                t = bass.ds(k * U * TPB, U * TPB)
                pool.wait_ge(var_done, k + 1)
                nc.gpsimd.tensor_tensor(rstd[:, t], vare[:, t], minus_half[:], ALU.pow).then_inc(rstd_done, 1)

            def add_bias(k, q):
                b = k * U + q
                ts = bass.ds(b * TPB, TPB)
                pool.wait_ge(xn_done, TPB * (b + 1))
                pool.sem_inc(passed, 1)
                nc.gpsimd.tensor_tensor(acc[:, ts, :], acc[:, ts, :], bout[:, None, :].to_broadcast([P, TPB, D]),
                                        ALU.add).then_inc(bout_done, 1)
                pool.wait_ge(bout_done, b + 1)
                pool.wait_ge(skip_done, b + 1)
                pool.sem_inc(passed, 1)
                nc.gpsimd.tensor_tensor(acc[:, ts, :], acc[:, ts, :], skipped[q], ALU.add).then_inc(bias_done, 1)
            first(0, 0)
            first(1, 0)
            pool.wait_ge(consts_in, 16 * N_CONSTS)
            add_bias(0, 0)
            add_bias(0, 1)
            first(2, 0)
            add_bias(0, 2)
            add_bias(0, 3)
            first(3, 0)
            steps(pool, B, add_bias, done=U)

            pool.wait_ge(topsq_done, 1)
            nc.gpsimd.partition_all_reduce(maxsq[:], topsq[:], P, RMAX).then_inc(maxsq_done, 1)
            pool.wait_ge(b1max_done, 1)
            nc.gpsimd.partition_all_reduce(b1max[:], b1m[:], P, RMAX).then_inc(maxsq_done, 1)
            for w, (hi, lo) in enumerate(((w1h, w1l), (w2h, w2l))):
                pool.wait_ge(w_high, w + 1)
                nc.gpsimd.tensor_tensor(lo[:], wst[:, w, :], hi[:], ALU.subtract).then_inc(w_low, 1)

            for c in range(K):
                if c:
                    pool.wait_ge(scattered[0], 16 * T)
                nc.gpsimd.iota(row[:, :, D].bitcast(I32).rearrange("p (b j) -> p b j", j=TPB),
                               pattern=[[SEQ, B], [1, TPB]], base=c * TOK, channel_multiplier=TPB
                               ).then_inc(dest_done, 1)
                pool.wait_ge(dest_done, c + 1)
                if c == 0:
                    pool.wait_ge(pads_out, 16)
                    pool.wait_ge(pos_ready, 1)
                for t in range(T):
                    nc.gpsimd.indirect_dma_start(
                        grouped, bass.IndirectOffsetOnAxis(ap=pos[:, c, t:t + 1].bitcast(U32), axis=0),
                        row[:, t, :], None,
                        bounds_check=ROWS - 1, oob_is_err=False).then_inc(scattered[c], 16)

            def scatter(k, q):
                j, u = k * U + q, q % 2
                pool.wait_ge(y_done, j + 1)
                pool.wait_ge(goes_done, j + 1)
                pool.sem_inc(passed, 1)
                for h in range(HALF):
                    nc.gpsimd.indirect_dma_start(
                        expert_out, bass.IndirectOffsetOnAxis(ap=goes[:, q, h:h + 1].bitcast(U32), axis=0),
                        ysb[u][:, h, :], None, bounds_check=K * TOK - 1, oob_is_err=False).then_inc(y_out[u], 16)
            steps(pool, N_TILES, scatter)

        @block.tensor
        def _(pe):
            pe.wait_ge(consts_in, 16 * N_CONSTS)
            pe.wait_ge(pool_const, 2)
            nc.tensor.transpose(ps[0:RANK, 0, 0:P], wdt1[:], ident[:])
            nc.tensor.transpose(ps[:, 1, 0:E * CH], b1rows[:], ident[0:E * CH, 0:E * CH]).then_inc(pe_setup, 1)
            pe.wait_ge(act_setup, 1)
            nc.tensor.matmul(ps[:, 2, 0:P], wdt1T[:], wdt2[:], start=True, stop=True)
            nc.tensor.matmul(ps[:, 3, 0:1], wdt2[:], cols[0:RANK, 2:3], start=True, stop=True).then_inc(pe_setup, 1)
            pe.wait_ge(act_setup, 4)

            def logits(k, q):
                b, u = k * U + q, q % 2
                pe.wait_ge(xnT2_done, b + 1)
                for j in range(TPB):
                    mm = nc.tensor.matmul(ps[:, 2, bass.ds((b * TPB + j) * E, E)], xnT2[:, u, j:SEQ:TPB], wG[:],
                                          start=True, stop=True, skip_group_check=True)
                mm.then_inc(logits_done, 1)

            def turn(k, q):
                b, u = k * U + q, q % 2
                need(pe, xnT_done, b - 1)
                pe.wait_ge(xn_done, TPB * (b + 1))
                for j in range(TPB):
                    mm = nc.tensor.transpose(ps[:, u, j * P:(j + 1) * P], xn2[:, u, j, :], ident[:])
                mm.then_inc(turned, 1)
                if isinstance(k, int) and k == 0 and q == 0:
                    return
                logits(*((k, q - 1) if q else (k - 1, U - 1)))
            steps(pe, B, turn)
            logits(B // U - 1, U - 1)

            pe.wait_ge(gate_mask, 1)
            nc.tensor.matmul(ps[:, 3, :], before[:], mask16[:].rearrange("p t e -> p (t e)"), start=True, stop=True)
            nc.tensor.matmul(ps[:, 4, :], ones16[:], mask16[:].rearrange("p t e -> p (t e)"), start=True, stop=True
                             ).then_inc(ranked, 1)
            pe.wait_ge(p_ready, 1)
            for g in range(U):
                mm = nc.tensor.transpose(ps[:, 5, g * P:(g + 1) * P],
                                         gw[:, g * 16:(g + 1) * 16, :].rearrange("p t e -> p (t e)"), ident[:])
            mm.then_inc(p_turned, 1)

            def z(k, q):
                b, u = k * U + q, q % 2
                need(pe, relz_done, b - 1)
                need(pe, absz_done, b - 1)
                nc.tensor.matmul(ps[:, u, :], wdt[:], xnT[:, bass.ds(b, 1), :].rearrange("p a s -> p (a s)"),
                                 start=True, stop=True).then_inc(z_done, 1)
            pe.wait_ge(xnT_done, B)
            steps(pe, B, z)

            pe.wait_ge(b2_in, 16 * (T // U))
            pe.wait_ge(bias_done, B)
            pe.wait_ge(pos_ready, 1)

            def project(k, q):
                b, u = k * U + q, q % 2
                need(pe, acc_done, b - 1)
                if q == 0:
                    pe.wait_ge(pTs_done, k + 1)
                bank = ps[:, 6 + u, :]
                rows = slice(q * TPB * E, (q + 1) * TPB * E)
                nc.tensor.matmul(bank, pTs[rows, :], b2diag[rows].rearrange("p j d -> p (j d)"),
                                 start=True, stop=False, skip_group_check=True)
                nc.tensor.matmul(bank, ident[:], acc[:, bass.ds(b * TPB, TPB), :].rearrange("p j d -> p (j d)"),
                                 start=False, stop=False, skip_group_check=True)
                pe.wait_ge(ret_done, b + 1)
                for j in range(TPB):
                    mm = nc.tensor.matmul(ps[:, 6 + u, j * D:(j + 1) * D], ret[:, u, j:SEQ:TPB], wO[:],
                                          start=False, stop=(j == TPB - 1), skip_group_check=True)
                mm.then_inc(out_done, 1)

            def write_read(k, q):
                b, u = k * U + q, q % 2
                need(pe, content_done, b - 1)
                need(pe, ret_done, b - 1)
                xb = xnT[:, bass.ds(b, 1), :].rearrange("p a s -> p (a s)")
                nc.tensor.matmul(ps[:, 2 + u, :], wB[:], xb, start=True, stop=True)
                nc.tensor.matmul(ps[:, 4 + u, :], wC[:], xb, start=True, stop=True).then_inc(bc_done, 1)
                if isinstance(k, int) and k == 0 and q == 0:
                    return
                project(*((k, q - 1) if q else (k - 1, U - 1)))
            steps(pe, B, write_read)
            project(B // U - 1, U - 1)

            pe.wait_ge(acc_done, B)
            pe.wait_ge(w_low, 2)
            pe.wait_ge(w_high, 2)
            pe.wait_ge(tile_ready, 1)

            def turn_tile(k, q):
                j, u = k * FU + q, q % 2
                pe.wait_ge(xs_in[q % U], 16 * (k * (FU // U) + q // U + 1))
                for h in range(HALF):
                    mm = nc.tensor.transpose(ps[:, u, h * P:(h + 1) * P], xs[q % U][:, h, 0:D], ident[:])
                mm.then_inc(xt_done, 1)

            def weights_of(k, q):
                return pe.value_load(tile_column[0:1, bass.ds(k * FU + q, 1)], min_val=0, max_val=(E - 1) * FF)

            def layer1(k, q, w0):
                j, u = k * FU + q, q % 2
                pe.wait_ge(xl_done, j + 1)
                for c in range(CH):
                    o = ps[:, 2 + 2 * u + c // 2, (c % 2) * TILE:(c % 2 + 1) * TILE]
                    hi, lo = (w[:, bass.ds(w0 + c * P, P)] for w in (w1h, w1l))
                    nc.tensor.matmul(o, hi, xh[q % U], start=True, stop=False)
                    nc.tensor.matmul(o, hi, xl[q % U], start=False, stop=False)
                    nc.tensor.matmul(o, lo, xh[q % U], start=False, stop=True).then_inc(l1_done, 1)

            def layer2(k, q, w0):
                j, u = k * FU + q, q % 2
                pe.wait_ge(hl_done, 2 * (j + 1))
                for h in range(HALF):
                    o = ps[:, 6 + u, h * D:(h + 1) * D]
                    for c in range(CH):
                        hi, lo = (w[:, bass.ds(w0 + c * D, D)] for w in (w2h, w2l))
                        a, b = (v[u][:, c, h * P:(h + 1) * P] for v in (hh, hl))
                        nc.tensor.matmul(o, a, hi, start=(c == 0), stop=False, skip_group_check=True)
                        nc.tensor.matmul(o, a, lo, start=False, stop=False, skip_group_check=True)
                        mm = nc.tensor.matmul(o, b, hi, start=False, stop=(c == CH - 1), skip_group_check=True)
                mm.then_inc(l2_done, 1)

            column = [None, None]

            def tile_step(k, q):
                if q == 0:
                    if not (isinstance(k, int) and k == 0):
                        column[0] = weights_of(k - 1, FU - 1)
                column[1] = weights_of(k, q)
                layer1(k, q, column[1])
                if not (isinstance(k, int) and k * FU + q + 2 >= N_TILES):
                    turn_tile(*((k, q + 2) if q + 2 < FU else (k + 1, q + 2 - FU)))
                if not (isinstance(k, int) and k == 0 and q == 0):
                    layer2(*((k, q - 1) if q else (k - 1, FU - 1)), column[0])
                column[0] = column[1]
            turn_tile(0, 0)
            turn_tile(0, 1)
            steps(pe, N_TILES, tile_step, FU)
            layer2((N_TILES - 1) // FU, (N_TILES - 1) % FU, column[0])

        @block.scalar
        def _(act):
            def col(i, v, n=P):
                act.dma_start(cols[0:n, i:i + 1], v.rearrange("(a b) -> a b", b=1)).then_inc(consts_in, 16)
            for i, v, n in ((0, b_B, P), (1, b_C, P), (2, b_dt1, RANK), (3, b_dt2, P), (4, omega, P)):
                col(i, v, n)
            for dst, src in ((wB, W_B), (wC, W_C), (wO, W_out), (wG, Wg), (wdt1, W_dt1), (wdt2, W_dt2)):
                act.dma_start(dst[:], src).then_inc(consts_in, 16)
            act.dma_start(b1rows[:], b1.rearrange("e (c f) -> (e c) f", f=P)).then_inc(consts_in, 16)
            act.dma_start(bout[:], b_out.partition_broadcast(P)).then_inc(consts_in, 16)
            act.dma_start(skip[:], D_skip.partition_broadcast(P)).then_inc(consts_in, 16)
            act.dma_start(bgate[:], bg.partition_broadcast(P)).then_inc(consts_in, 16)
            act.wait_ge(pe_setup, 1)
            nc.scalar.copy(wdt1T[:], ps[0:RANK, 0, 0:P]).then_inc(act_setup, 1)
            nc.scalar.copy(b1T[:], ps[:, 1, 0:E * CH]).then_inc(act_setup, 1)
            act.wait_ge(pe_setup, 2)
            nc.scalar.copy(wdt[:], ps[:, 2, 0:P]).then_inc(act_setup, 1)
            nc.scalar.activation(cols[:, 5:6], ps[:, 3, 0:1], ACT.Identity, bias=cols[:, 3:4]).then_inc(act_setup, 1)

            def keep(k, q):
                b, u = k * U + q, q % 2
                act.wait_ge(turned, b + 1)
                need(act, logits_done, b - 1)
                nc.scalar.copy(row[:, bass.ds(b * TPB, TPB), 0:D], xn2[:, u]).then_inc(row_done, 1)
                t = ps[:, u, :].rearrange("p (j n) -> p n j", j=TPB)
                nc.scalar.copy(xnT2[:, u, :].rearrange("p (n j) -> p n j", j=TPB), t).then_inc(xnT2_done, 1)
                nc.scalar.copy(xnT[:, bass.ds(b, 1), :].rearrange("p a (n j) -> p (a n) j", j=TPB), t
                               ).then_inc(xnT_done, 1)
                if not (isinstance(k, int) and k == 0):
                    square(b - U)

            def square(piece):
                nc.scalar.activation(squares[:, bass.ds(piece, 1), :].rearrange("p a n -> p (a n)"),
                                     shared[:, bass.ds(piece * SEQ, SEQ)], ACT.Square,
                                     accum_out=sumsq[:, bass.ds(piece, 1)]).then_inc(sumsq_done, 1)

            def weights_in():
                act.wait_ge(w_in, 32)
            steps(act, B, keep, between=weights_in)
            for piece in range(B - U, B):
                square(piece)

            act.wait_ge(gate_max, 1)
            nc.scalar.activation(pr[:], lg[:], ACT.Exp).then_inc(gate_exp, 1)
            act.wait_ge(scales_done, 1)
            act.wait_ge(sumsq_done, B)
            for w, hi in enumerate((w1h, w2h)):
                nc.scalar.activation(wst[:, w, :], wst[:, w, :], ACT.Copy, scale=scl[:, w:w + 1]).then_inc(w_scaled, 1)
                act.wait_ge(w_scaled, w + 1)
                nc.scalar.copy(hi[:], wst[:, w, :]).then_inc(w_high, 1)
            act.wait_ge(p_turned, 1)
            nc.scalar.copy(pT[:].rearrange("p g n -> p (g n)"), ps[:, 5, :]).then_inc(pT_done, 1)

            nc.scalar.preload_act_table_set("natural_log_exp_and_others")
            act.wait_ge(tile_ready, 1)

            def softplus(k, q):
                b, u = k * U + q, q % 2
                act.wait_ge(z_done, b + 1)
                need(act, exp_done, b - 1)
                nc.scalar.activation(absz[:, u, :], ps[:, u, :], ACT.Abs, bias=cols[:, 5:6]).then_inc(absz_done, 1)
                need(act, sum_done, b - 1)
                nc.scalar.activation(relz[:, u, :], ps[:, u, :], ACT.Relu, bias=cols[:, 5:6]).then_inc(relz_done, 1)
                act.wait_ge(absz_done, b + 1)
                need(act, ln_done, b - 1)
                nc.scalar.activation(ex[:, u, :], absz[:, u, :], ACT.Exp, scale=-1.0).then_inc(exp_done, 1)
                act.wait_ge(exp_done, b + 1)
                nc.scalar.activation(lnz[:, u, :], ex[:, u, :], ACT.Ln, bias=1.0).then_inc(ln_done, 1)
            steps(act, B, softplus)

            nc.scalar.preload_act_table(ACT.Sin)

            def waves(k, q):
                b, u = k * U + q, q % 2
                act.wait_ge(phase_done, b + 1)
                need(act, q2_done, b - 1)
                need(act, q1_done, b - 1)
                f = phase[:, bass.ds(b, 1), :].rearrange("p a s -> p (a s)")
                nc.scalar.activation(sn[:, u, :], f, ACT.Sin, scale=TWO_PI).then_inc(sin_done, 1)
                nc.scalar.activation(ab[:, u, :], f, ACT.Abs).then_inc(ab_done, 1)
                act.wait_ge(ab_done, b + 1)
                nc.scalar.activation(cs[:, u, :], ab[:, u, :], ACT.Sin, scale=-TWO_PI, bias=cols[:, 7:8]
                                     ).then_inc(cos_done, 1)
                if q == 0:
                    need(act, out_done, b)
                    nc.scalar.copy(pTs[:], pT[:, bass.ds(k, 1), :].rearrange("p a n -> p (a n)")).then_inc(pTs_done, 1)
                if not (isinstance(k, int) and k == 0 and q == 0):
                    keep_out(*((k, q - 1) if q else (k - 1, U - 1)))

            def keep_out(k, q):
                b, u = k * U + q, q % 2
                act.wait_ge(out_done, b + 1)
                nc.scalar.copy(acc[:, bass.ds(b * TPB, TPB), :].rearrange("p j d -> p (j d)"), ps[:, 6 + u, :]
                               ).then_inc(acc_done, 1)
            act.wait_ge(phase_done, B)
            act.wait_ge(ln_done, B)
            act.wait_ge(pT_done, 1)
            steps(act, B, waves)
            keep_out(B // U - 1, U - 1)

            nc.scalar.preload_act_table(ACT.Gelu)
            act.wait_ge(ab_done, B)
            act.wait_ge(cos_done, B)

            def high(k, q):
                j, u = k * FU + q, q % 2
                act.wait_ge(xt_done, j + 1)
                need(act, l1_done, CH * (j - 3))
                nc.scalar.copy(xh[q % U], ps[:, u, 0:TILE]).then_inc(xh_done, 1)

            def gelu(k, q):
                j, u = k * FU + q, q % 2
                e = act.value_load(tile_expert[0:1, bass.ds(j, 1)], min_val=0, max_val=E - 1)
                need(act, hl_done, 2 * (j - 1))
                for c in range(CH):
                    act.wait_ge(l1_done, CH * j + 2 * (c // 2) + 2)
                    nc.scalar.activation(gel[u][:, c, :], ps[:, 2 + 2 * u + c // 2, (c % 2) * TILE:(c % 2 + 1) * TILE],
                                         ACT.Gelu, bias=b1T[:, bass.ds(e * CH + c, 1)], scale=scl[:, 2:3]
                                         ).then_inc(gelu_done, 1)

            def result(k, q):
                j, u = k * FU + q, q % 2
                act.wait_ge(l2_done, j + 1)
                need(act, y_out[u], 32 * (FU // 2 * k + q // 2))
                nc.scalar.activation(ysb[u].rearrange("p h d -> p (h d)"), ps[:, 6 + u, 0:HALF * D], ACT.Copy,
                                     scale=scl[:, 4:5]).then_inc(y_done, 1)

            def tile_step(k, q):
                gelu(k, q)
                if not (isinstance(k, int) and k * FU + q + 2 >= N_TILES):
                    high(*((k, q + 2) if q + 2 < FU else (k + 1, q + 2 - FU)))
                if not (isinstance(k, int) and k == 0 and q == 0):
                    result(*((k, q - 1) if q else (k - 1, FU - 1)))
            act.wait_ge(tile_ready, 1)
            high(0, 0)
            high(0, 1)
            steps(act, N_TILES, tile_step, FU)
            result((N_TILES - 1) // FU, (N_TILES - 1) % FU)

            for b in range(B):
                act.wait_ge(add1_done, b + 1)
                act.dma_start(out_seq[:, b], acc[:, b * TPB:(b + 1) * TPB, :]).then_inc(stored, 16)
            act.wait_ge(stored, 16 * B)

        @block.vector
        def _(dve):
            def norm(k, q):
                b, u = k * U + q, q % 2
                need(dve, row_done, b - 1)
                need(dve, turned, b - 1)
                need(dve, skip_done, b - 1)
                dve.wait_ge(rstd_done, k + 1)
                for j in range(TPB):
                    t = b * TPB + j
                    nc.vector.tensor_scalar(xn2[:, u, j, :], acc[:, bass.ds(t, 1), :].rearrange("p a d -> p (a d)"),
                                            mean[:, bass.ds(t, 1)], rstd[:, bass.ds(t, 1)], ALU.subtract, ALU.mult
                                            ).then_inc(xn_done, 1)
                need(dve, bias_done, b - U + 1)
                dve.wait_ge(xn_done, TPB * (b + 1))
                nc.vector.tensor_tensor(skipped[q], xn2[:, u], skip[:, None, :].to_broadcast([P, TPB, D]), ALU.mult
                                        ).then_inc(skip_done, 1)

            def moments(k, _):
                dve.wait_ge(x_in[k], 16)
                for i in range(U * TPB):
                    t = k * U * TPB + i
                    mm = nc.vector.bn_stats(stats[:, bass.ds(t, 1), :].rearrange("p a c -> p (a c)"),
                                            acc[:, bass.ds(t, 1), :].rearrange("p a d -> p (a d)"))
                mm.then_inc(stats_done, 1)
                dve.wait_ge(stats_done, k + 1)
                ts = bass.ds(k * U * TPB, U * TPB)
                m_even, s_even, m_odd, s_odd = (stats[:, ts, i:i + 1].rearrange("p t a -> p (t a)") for i in (1, 2, 4, 5))
                nc.vector.tensor_tensor(mean[:, ts], m_even, m_odd, ALU.add)
                nc.vector.tensor_tensor(gap[:, ts], m_even, m_odd, ALU.subtract)
                nc.vector.tensor_tensor(vare[:, ts], s_even, s_odd, ALU.add).then_inc(moment, 1)
                dve.wait_ge(moment, 2 * k + 1)
                nc.vector.tensor_scalar(mean[:, ts], mean[:, ts], 0.5, None, ALU.mult)
                nc.vector.tensor_scalar(vare[:, ts], vare[:, ts], 1.0 / D, 1e-5, ALU.mult, ALU.add)
                nc.vector.scalar_tensor_tensor(out=gap[:, ts], in0=gap[:, ts], scalar=0.25, in1=gap[:, ts],
                                               op0=ALU.mult, op1=ALU.mult).then_inc(moment, 1)
                dve.wait_ge(moment, 2 * k + 2)
                nc.vector.tensor_tensor(vare[:, ts], vare[:, ts], gap[:, ts], ALU.add).then_inc(var_done, 1)

            moments(0, 0)
            moments(1, 0)
            dve.wait_ge(consts_in, 16 * N_CONSTS)
            norm(0, 0)
            norm(0, 1)
            moments(2, 0)
            norm(0, 2)
            norm(0, 3)
            moments(3, 0)
            steps(dve, B, norm, done=U)

            V = nc.vector

            n_gate = [0]

            def link(ins):
                n_gate[0] += 1
                ins.then_inc(gate, 1)
                dve.wait_ge(gate, n_gate[0])

            def over_e(v):
                return v[:, :, None].to_broadcast([P, T, E])

            dve.wait_ge(act_setup, 4)
            V.tensor_reduce(b1m[:], b1T[:], AX, ALU.max, apply_absolute_value=True).then_inc(b1max_done, 1)
            dve.wait_ge(sumsq_done, B)
            V.tensor_reduce(topsq[:], sumsq[:].rearrange("p (w n) -> p w n", w=2), AX, ALU.max).then_inc(topsq_done, 1)
            dve.wait_ge(logits_done, B)
            dve.wait_ge(bias_done, B)
            dve.wait_ge(pool_const, 2)
            dve.wait_ge(consts_in, 16 * N_CONSTS)
            link(V.memset(cols[:, 7:8], 1.5707963))
            link(V.tensor_scalar(cols[:, 6:7], cols[:, 4:5], 1.0 / 6.283185307179586, None, ALU.mult))
            link(V.tensor_tensor(lg[:], ps[:, 2, :].rearrange("p (t e) -> p t e", e=E),
                                 bgate[:, None, :].to_broadcast([P, T, E]), ALU.add))
            link(V.tensor_reduce(mx[:], lg[:], AX, ALU.max))
            V.tensor_tensor(lg[:], lg[:], over_e(mx[:]), ALU.subtract).then_inc(gate_max, 1)

            n_scale = [0]

            def scale(ins):
                n_scale[0] += 1
                ins.then_inc(scale_step, 1)
                dve.wait_ge(scale_step, n_scale[0])

            dve.wait_ge(maxsq_done, 2)
            scale(V.tensor_scalar(maxsq[:], maxsq[:], 2.0 ** -100, 2.0 ** 100, ALU.max, ALU.min))
            scale(V.tensor_scalar(pwi, maxsq[:].bitcast(I32), 23, None, ALU.logical_shift_right))
            scale(V.tensor_scalar(pwi, pwi, 129, None, ALU.add))
            scale(V.tensor_scalar(pwi, pwi, 1, 23, ALU.logical_shift_right, ALU.logical_shift_left))
            scale(V.scalar_tensor_tensor(out=pw[:, 2:3], in0=pw[:, 0:1], scalar=2048.0, in1=b1max[:],
                                         op0=ALU.mult, op1=ALU.add))
            scale(V.tensor_scalar(pw[:, 3:4].bitcast(I32), pw[:, 2:3].bitcast(I32), 0x7F800000, None, ALU.bitwise_and))
            scale(V.reciprocal(scl[:, 5:7], pw[:, 0:2]))
            scale(V.reciprocal(scl[:, 7:8], pw[:, 3:4]))
            scale(V.tensor_scalar(scl[:, 0:2], scl[:, 5:7], 2.0 ** 15, None, ALU.mult))
            scale(V.tensor_scalar(scl[:, 2:3], pw[:, 0:1], 2.0 ** -15, None, ALU.mult))
            scale(V.tensor_scalar(scl[:, 3:4], scl[:, 7:8], 2.0 ** 14, None, ALU.mult))
            V.scalar_tensor_tensor(out=scl[:, 4:5], in0=pw[:, 3:4], scalar=2.0 ** -29, in1=pw[:, 1:2],
                                   op0=ALU.mult, op1=ALU.mult).then_inc(scales_done, 1)

            dve.wait_ge(gate_exp, 1)
            link(V.tensor_reduce(sm[:], pr[:], AX, ALU.add))
            link(V.reciprocal(sm[:], sm[:]))
            link(V.tensor_tensor(pr[:], pr[:], over_e(sm[:]), ALU.mult))
            rest = pr
            for c, one_hot in ((0, g1), (1, g2)):
                link(V.tensor_reduce(m12[:, c, :], rest[:], AX, ALU.max))
                link(V.tensor_tensor(one_hot[:], rest[:], over_e(m12[:, c, :]), ALU.is_equal))
                link(V.tensor_tensor(one_hot[:], one_hot[:], desc[:, None, :].to_broadcast([P, T, E]), ALU.mult))
                link(V.tensor_reduce(mx[:], one_hot[:], AX, ALU.max))
                link(V.tensor_tensor(one_hot[:], one_hot[:], over_e(mx[:]), ALU.is_equal))
                if c == 0:
                    rest = lg
                    link(V.scalar_tensor_tensor(out=lg[:].rearrange("p t e -> p (t e)"),
                                                in0=g1[:].rearrange("p t e -> p (t e)"), scalar=-2.0,
                                                in1=pr[:].rearrange("p t e -> p (t e)"), op0=ALU.mult, op1=ALU.add))
            V.tensor_tensor(mask16[:], g1[:], g2[:], ALU.add).then_inc(gate_mask, 1)
            dve.wait_ge(gate_mask, 1)
            link(V.tensor_tensor(den[:], m12[:, 0, :], m12[:, 1, :], ALU.add))
            link(V.tensor_scalar(den0[:], den[:], 0.0, None, ALU.is_equal))
            link(V.tensor_tensor(den[:], den[:], den0[:], ALU.add))
            link(V.reciprocal(den[:], den[:]))
            link(V.tensor_tensor(gk[:, 0, :], m12[:, 0, :], den[:], ALU.mult))
            link(V.tensor_tensor(gk[:, 1, :], m12[:, 1, :], den[:], ALU.mult))
            link(V.tensor_tensor(pr[:], pr[:], mask16[:], ALU.mult))
            V.tensor_tensor(gw[:], pr[:], over_e(den[:]), ALU.mult).then_inc(p_ready, 1)
            dve.wait_ge(p_ready, 1)

            dve.wait_ge(ranked, 1)
            dve.wait_ge(row_done, B)
            dve.wait_ge(turned, B)
            link(V.tensor_copy(tot, ps[:, 4, :].rearrange("p (t e) -> p e t", e=E)))
            for e in range(E):
                i = V.tensor_tensor_scan(cum[:, e, :], tot[:, e, :], zeros[:, 0:T], 0.0, ALU.add, ALU.add)
            link(i)
            count, tiles, ends, start = (sizes[:, i, :] for i in range(4))
            link(V.tensor_copy(count, cum[:, :, T - 1]))
            link(V.tensor_scalar(tiles, count, 1.0 / TILE, (TILE - 1.0) / TILE - 0.5 + 0.5 / TILE, ALU.mult, ALU.add))
            link(V.tensor_scalar(tiles, tiles, ROUND, None, ALU.add))
            link(V.tensor_scalar(tiles, tiles, ROUND, None, ALU.subtract))
            link(V.tensor_tensor_scan(ends, tiles, zeros[:, 0:E], 0.0, ALU.add, ALU.add))
            link(V.tensor_tensor(start, ends, tiles, ALU.subtract))
            link(V.tensor_scalar(start, start, float(TILE), None, ALU.mult))
            link(V.tensor_tensor(cum, cum, tot, ALU.subtract))
            link(V.tensor_tensor(cum, cum, start[:, :, None].to_broadcast([P, E, T]), ALU.add))
            link(V.tensor_tensor(lg[:], ps[:, 3, :].rearrange("p (t e) -> p t e", e=E),
                                 cum.rearrange("p e t -> p t e"), ALU.add))
            for c, one_hot in ((0, g1), (1, g2)):
                link(V.tensor_tensor(one_hot[:], one_hot[:], lg[:], ALU.mult))
                link(V.tensor_reduce(posf[:, c, :], one_hot[:], AX, ALU.add))
            V.tensor_copy(pos[:], posf[:]).then_inc(pos_ready, 1)
            link(V.tensor_tensor(past, jrow[:, :, None].to_broadcast([P, N_TILES, E]),
                                 ends[:, None, :].to_broadcast([P, N_TILES, E]), ALU.is_ge))
            link(V.tensor_reduce(tile_e[:], past, AX, ALU.add))
            V.tensor_scalar(tile_expert[:], tile_e[:], float(E - 1), None, ALU.min)
            V.tensor_scalar(tile_column[:], tile_e[:], float(E - 1), float(FF), ALU.min, ALU.mult).then_inc(tile_ready, 1)

            w_turn = cols[:, 6:7]

            def accumulate(k, q):
                b, u = k * U + q, q % 2
                dve.wait_ge(ln_done, b + 1)
                dve.wait_ge(relz_done, b + 1)
                need(dve, phase_done, b)
                V.tensor_tensor_scan(steps_sum, relz[:, u, :], lnz[:, u, :], 0.0, ALU.add, ALU.add
                                     ).then_inc(sum_done, 1)
                dve.wait_ge(sum_done, b + 1)
                V.tensor_scalar(turns, steps_sum, w_turn, ROUND, ALU.mult, ALU.add).then_inc(t1, 1)
                dve.wait_ge(t1, b + 1)
                V.tensor_scalar(whole, turns, ROUND, None, ALU.subtract).then_inc(t2, 1)
                dve.wait_ge(t2, b + 1)
                V.scalar_tensor_tensor(out=phase[:, bass.ds(b, 1), :].rearrange("p a s -> p (a s)"),
                                       in0=steps_sum, scalar=w_turn, in1=whole, op0=ALU.mult, op1=ALU.subtract
                                       ).then_inc(phase_done, 1)

            dve.wait_ge(p_turned, 1)
            dve.wait_ge(w_low, 2)
            steps(dve, B, accumulate)

            def recall(k, q):
                b, u = k * U + q, q % 2
                xb = xnT[:, bass.ds(b, 1), :].rearrange("p a s -> p (a s)")
                dve.wait_ge(bc_done, b + 1)
                need(dve, ret_done, b)
                V.scalar_tensor_tensor(out=content, in0=ps[:, 2 + u, :], scalar=cols[:, 0:1], in1=xb,
                                       op0=ALU.add, op1=ALU.mult).then_inc(content_done, 1)
                dve.wait_ge(content_done, b + 1)
                dve.wait_ge(cos_done, b + 1)
                V.tensor_tensor(p1, content, cs[:, u, :], ALU.mult).then_inc(p1_done, 1)
                V.tensor_tensor(p2, content, sn[:, u, :], ALU.mult).then_inc(p2_done, 1)
                dve.wait_ge(p1_done, b + 1)
                V.tensor_tensor_scan(m1, p1, zeros[:], 0.0, ALU.add, ALU.add).then_inc(m1_done, 1)
                dve.wait_ge(p2_done, b + 1)
                V.tensor_tensor_scan(m2[:], p2, zeros[:], 0.0, ALU.add, ALU.add).then_inc(m2_done, 1)
                dve.wait_ge(m1_done, b + 1)
                V.tensor_tensor(q1, m1, cs[:, u, :], ALU.mult).then_inc(q1_done, 1)
                dve.wait_ge(m2_done, b + 1)
                V.tensor_tensor(q2, m2[:], sn[:, u, :], ALU.mult).then_inc(q2_done, 1)
                dve.wait_ge(q2_done, b + 1)
                dve.wait_ge(q1_done, b + 1)
                V.tensor_tensor(qs, q1, q2, ALU.add).then_inc(qs_done, 1)
                dve.wait_ge(qs_done, b + 1)
                need(dve, out_done, b - 1)
                V.scalar_tensor_tensor(out=ret[:, u, :], in0=ps[:, 4 + u, :], scalar=cols[:, 1:2], in1=qs,
                                       op0=ALU.add, op1=ALU.mult).then_inc(ret_done, 1)
            dve.wait_ge(phase_done, B)
            steps(dve, B, recall)

            def low(k, q):
                j, u = k * FU + q, q % 2
                dve.wait_ge(xh_done, j + 1)
                need(dve, l1_done, CH * (j - 3))
                V.tensor_tensor(xl[q % U], ps[:, u, 0:TILE], xh[q % U], ALU.subtract).then_inc(xl_done, 1)

            def keep_goes(k, q):
                dve.wait_ge(xs_in[q % U], 16 * (k * (FU // U) + q // U + 1))
                need(dve, y_out[q % 2], 32 * (FU // 2 * k + q // 2 - 1))
                V.tensor_copy(goes[:, q % U, :], xs[q % U][:, :, D].bitcast(I32)).then_inc(goes_done, 1)

            def hidden(k, q):
                j, u = k * FU + q, q % 2
                need(dve, l2_done, j - 1)
                for i in range(2):
                    dve.wait_ge(gelu_done, CH * j + 2 * i + 2)
                    g, a, b = (v[u][:, 2 * i:2 * i + 2, :].rearrange("p c n -> p (c n)") for v in (gel, hh, hl))
                    V.tensor_scalar(a, g, scl[:, 3:4], None, ALU.mult).then_inc(hh_done, 1)
                    dve.wait_ge(hh_done, 2 * j + i + 1)
                    V.scalar_tensor_tensor(out=b, in0=g, scalar=scl[:, 3:4], in1=a, op0=ALU.mult, op1=ALU.subtract
                                           ).then_inc(hl_done, 1)

            def tile_step(k, q):
                if not (isinstance(k, int) and k * FU + q + 1 >= N_TILES):
                    keep_goes(*((k, q + 1) if q + 1 < FU else (k + 1, 0)))
                hidden(k, q)
                if not (isinstance(k, int) and k * FU + q + 2 >= N_TILES):
                    low(*((k, q + 2) if q + 2 < FU else (k + 1, q + 2 - FU)))
            low(0, 0)
            low(0, 1)
            keep_goes(0, 0)
            steps(dve, N_TILES, tile_step, FU)

            dve.wait_ge(acc_done, B)
            for b in range(B):
                r = b % (B // 2)
                dve.wait_ge(back_in[r], 16 * (b // (B // 2) + 1))
                for c in range(K):
                    if c:
                        dve.wait_ge(add0_done, b + 1)
                    for j in range(TPB):
                        t = b * TPB + j
                        i = V.scalar_tensor_tensor(out=acc[:, t, :], in0=back[:, r, c, j * D:(j + 1) * D],
                                                   scalar=gk[:, c, t:t + 1], in1=acc[:, t, :],
                                                   op0=ALU.mult, op1=ALU.add)
                    i.then_inc((add0_done, add1_done)[c], 1)


_INS = ["x", "W_B", "b_B", "W_C", "b_C", "W_dt1", "b_dt1", "W_dt2", "b_dt2", "omega_base", "D", "W_out", "b_out"]
_FFN = ["W1", "b1", "W2", "b2", "Wg", "bg"]


def kernel(**inputs):
    import numpy as np
    import concourse.bacc as bacc
    from concourse import mybir as _mybir
    from concourse.bass_utils import run_bass_kernel_spmd

    nc = bacc.Bacc("TRN2", target_bir_lowering=False, num_devices=1)
    arrays, args = {}, []
    for name in ["L0_attn_" + n for n in _INS] + ["L0_ffn_" + n for n in _FFN]:
        a = np.ascontiguousarray(inputs[name])
        if name == "L0_attn_x":
            a = a.reshape(TOK, D)
        arrays["in_" + name] = a
        args.append(nc.dram_tensor("in_" + name, a.shape, _mybir.dt.from_np(a.dtype), kind="ExternalInput").ap())
    out = nc.dram_tensor("out_0", (TOK, D), F32, kind="ExternalOutput").ap()
    program(nc, *args, out)
    r = run_bass_kernel_spmd(nc, [arrays], core_ids=[0])
    return r.results[0]["out_0"].reshape(B, SEQ, D)
```

```python
from contextlib import ExitStack

import concourse.bass as bass
from concourse import mybir

ALU = mybir.AluOpType
ACT = mybir.ActivationFunctionType
F32 = mybir.dt.float32
F16 = mybir.dt.float16
BF16 = mybir.dt.bfloat16
I32 = mybir.dt.int32
U32 = mybir.dt.uint32
AX = mybir.AxisListType.X
RMAX = bass.bass_isa.ReduceOp.max

P = 128
B, SEQ, D = 16, 512, 128
TOK = B * SEQ
TPB = SEQ // P
T = B * TPB
E, FF, K = 8, 512, 2
CH = FF // P
RANK = 32
TILE = 512
GROUPS = TILE // P
N_TILES = K * TOK // TILE + E - 1
ROWS = N_TILES * TILE
ROW = D + 2
NOWHERE = 65535
ROUND = 1.5 * 2.0 ** 23
TWO_PI = 6.283185
U = 4


def need(eng, sem, count):
    if isinstance(count, int) and count <= 0:
        return
    eng.wait_ge(sem, count)


def steps(eng, n, body, unroll=U, peel=1, between=None, done=0):
    for j in range(done, peel * unroll):
        body(j // unroll, j % unroll)
    if between:
        between()
    with eng.Fori(peel, n // unroll) as k:
        for q in range(unroll):
            body(k, q)
    for j in range(n // unroll * unroll, n):
        body(j // unroll, j % unroll)


def program(nc, x, W_B, b_B, W_C, b_C, W_dt1, b_dt1, W_dt2, b_dt2, omega, D_skip, W_out, b_out,
            W1, b1, W2, b2, Wg, bg, out):
    with ExitStack() as ctx:
        def sb(name, shape, dt=F32):
            return ctx.enter_context(nc.sbuf_tensor(name, shape, dt))

        def sem(name):
            return ctx.enter_context(nc.semaphore(name))

        grouped = nc.dram_tensor("grouped", (ROWS, ROW), F32, kind="Internal").ap()

        x_seq = x.rearrange("(b p j) d -> p b j d", p=P, j=TPB)
        out_seq = out.rearrange("(b p j) d -> p b j d", p=P, j=TPB)

        ps = ctx.enter_context(nc.psum_tensor("ps", [P, 8, 512], F32))

        acc = sb("acc", [P, T, D])
        row = sb("row", [P, T, ROW])
        xnT = sb("xnT", [P, B, SEQ])
        shared = sb("shared", [P, B * SEQ])
        w1 = sb("w1", [P, 2 * E * FF], F16)
        w1h, w1l = w1[:, 0:E * FF], w1[:, E * FF:]
        w2h = sb("w2h", [P, E * FF], F16)
        w2l = sb("w2l", [P, E * FF], F16)
        ident = sb("ident", [P, P])
        before = sb("before", [P, P], BF16)
        ones16 = sb("ones16", [P, P], BF16)
        wB = sb("wB", [P, D])
        wC = sb("wC", [P, D])
        wO = sb("wO", [P, D])
        wG = sb("wG", [P, E])
        wdt1 = sb("wdt1", [P, RANK])
        wdt1T = sb("wdt1T", [RANK, P])
        wdt2 = sb("wdt2", [RANK, P])
        wdt = sb("wdt", [P, P])
        cols = sb("cols", [P, 8])
        bout = sb("bout", [P, D])
        first_row = sb("first_row", [P, P])
        skip = sb("skip", [P, D])
        bgate = sb("bgate", [P, E])
        b1rows = sb("b1rows", [E * CH, P])
        b1T = sb("b1T", [P, E * CH])
        b2diag = sb("b2diag", [P, TPB, D])
        pT = sb("pT", [P, U, P])
        pTs = sb("pTs", [P, P])
        padrow = sb("padrow", [P, ROW])
        maxsq = sb("maxsq", [P, 2])
        pw = sb("pw", [P, 4])
        b1m = sb("b1m", [P, 1])
        b1max = sb("b1max", [P, 1])
        scl = sb("scl", [P, 8])
        xn2 = sb("xn2", [P, 2, TPB, D])
        xnT2 = sb("xnT2", [P, 2, SEQ])
        mean = sb("mean", [P, T])
        vare = sb("vare", [P, T])
        gap = sb("gap", [P, T])
        rstd = sb("rstd", [P, T])
        pwi = pw[:, 0:2].bitcast(I32)
        minus_half = sb("minus_half", [P, U * TPB])
        accumulated = sb("accumulated", [P, SEQ])
        scale_y = sb("scale_y", [P, U, GROUPS])
        goes = sb("goes", [P, U, GROUPS], I32)
        lg = sb("lg", [P, T, E])
        pr = sb("pr", [P, T, E])
        gw = sb("gw", [P, T, E])
        g1 = sb("g1", [P, T, E])
        g2 = sb("g2", [P, T, E])
        stats = g2[:].rearrange("p t e -> p (t e)")[:, 0:T * 6].rearrange("p (t c) -> p t c", c=6)
        gates = g2
        mask16 = sb("mask16", [P, T, E], BF16)
        mx, sm = gap, vare
        m12 = sb("m12", [P, K, T])
        gk = sb("gk", [P, K, T])
        den = sb("den", [P, T])
        den0 = sb("den0", [P, T])
        pos = sb("pos", [P, K, T], I32)
        posf = sb("posf", [P, K, T])
        desc = sb("desc", [P, E])
        jrow = sb("jrow", [P, N_TILES])
        skipped = [v[:].rearrange("p t e -> p (t e)").rearrange("p (j d) -> p j d", j=TPB) for v in (lg, pr, gw, g1)]
        tot, cum = (xn2[:, u].rearrange("p j d -> p (j d)").rearrange("p (e t) -> p e t", e=E) for u in range(2))
        zeros = sb("zeros", [P, SEQ])
        sizes = sb("sizes", [P, 8, E])
        past = gw[:].rearrange("p t e -> p (t e)")[:, 0:N_TILES * E].rearrange("p (n e) -> p n e", e=E)
        tile_e = sb("tile_e", [P, N_TILES])
        tile_expert = sb("tile_expert", [P, N_TILES], I32)
        tile_column = sb("tile_column", [P, N_TILES], I32)
        def flat(v):
            return v[:].rearrange("p a b -> p (a b)")

        absz, relz = xn2[:].rearrange("p u j d -> p u (j d)"), xnT2
        ex = sb("ex", [P, 2, SEQ])
        lnz = sb("lnz", [P, 2, SEQ])
        ret = lnz
        steps_sum = accumulated[:], flat(g1)
        turns, whole = flat(pr), flat(gw)
        sn, ab, cs = absz, relz, ex
        content, p1, m1 = flat(g1), flat(g2), flat(lg)
        p2, m2 = turns, accumulated[:]
        q1, q2, qs = m1, m2, m1

        def cut(v, at, n, dt=F32):
            words = n * (2 if dt == F16 else 4) // 4
            w = v[:, at[0]:at[0] + words]
            at[0] += words
            return w.bitcast(dt) if dt != F32 else w

        spent, at, at_spent = row[:].rearrange("p t c -> p (t c)"), [0], [0]
        gel = [cut(shared, at, CH * TILE).rearrange("p (c n) -> p c n", c=CH) for _ in range(2)]
        hh = [cut(shared, at, CH * TILE, F16).rearrange("p (c n) -> p c n", c=CH) for _ in range(2)]
        hl = [cut(shared, at, CH * TILE, F16).rearrange("p (c n) -> p c n", c=CH) for _ in range(2)]
        xs = [cut(spent, at_spent, GROUPS * ROW).rearrange("p (h c) -> p h c", h=GROUPS) for _ in range(U)]
        xh = [cut(spent, at_spent, TILE, F16) for _ in range(U)]
        xl = [cut(spent, at_spent, TILE, F16) for _ in range(U)]
        ysb = [cut(spent, at_spent, GROUPS * D).rearrange("p (h d) -> p h d", h=GROUPS) for _ in range(2)]
        phase = shared[:].rearrange("p (b s) -> p b s", b=B)
        squares = w1[:].rearrange("p (b n) -> p b n", b=B)
        sumsq, topsq = den[:, 0:B], den0[:, 0:2]
        wst = shared[:].rearrange("p (w n) -> p w n", w=2)

        x_in = [sem(f"x_in{i}") for i in range(4)]
        consts_in, w_in, b2_in, pads_out = sem("consts_in"), sem("w_in"), sem("b2_in"), sem("pads_out")
        pool_const, dve_const = sem("pool_const"), sem("dve_const")
        pe_setup, dve_setup, act_setup = sem("pe_setup"), sem("dve_setup"), sem("act_setup")
        passed = sem("passed")
        stats_done, moment, var_done, rstd_done, xn_done = (sem(n) for n in (
            "stats_done", "moment", "var_done", "rstd_done", "xn_done"))
        turned, xnT2_done, xnT_done, logits_done = (sem(n) for n in (
            "turned", "xnT2_done", "xnT_done", "logits_done"))
        row_done, skip_done, skipped_added = (sem(n) for n in ("row_done", "skip_done", "skipped_added"))
        gate, gate_max, gate_exp, gate_mask, ranked, p_ready, p_turned, pT_done, pos_ready, tile_ready = (
            sem(n) for n in ("gate", "gate_max", "gate_exp", "gate_mask", "ranked", "p_ready", "p_turned",
                             "pT_done", "pos_ready", "tile_ready"))
        counts_used = sem("counts_used")
        dest_done, scattered = sem("dest_done"), [sem("scattered0"), sem("scattered1")]
        topsq_done = sem("topsq_done")
        sumsq_done, maxsq_done, scales_done, scale_step, b1max_done = (sem(n) for n in (
            "sumsq_done", "maxsq_done", "scales_done", "scale_step", "b1max_done"))
        w_scaled, w_high, w_low = sem("w_scaled"), sem("w_high"), sem("w_low")
        z_done, absz_done, relz_done, exp_done, ln_done, sum_done, t1, t2, phase_done = (sem(n) for n in (
            "z_done", "absz_done", "relz_done", "exp_done", "ln_done", "sum_done", "t1", "t2", "phase_done"))
        bc_done, sin_done, ab_done, cos_done, content_done, p1_done, p2_done, m1_done, m2_done, q1_done, q2_done, \
            qs_done, ret_done, out_done, acc_done, pTs_done = (sem(n) for n in (
                "bc_done", "sin_done", "ab_done", "cos_done", "content_done", "p1_done", "p2_done", "m1_done",
                "m2_done", "q1_done", "q2_done", "qs_done", "ret_done", "out_done", "acc_done", "pTs_done"))
        xs_in = [sem(f"xs_in{i}") for i in range(U)]
        xt_done, xh_done, xl_done, l1_done, gelu_done, hh_done, hl_done, l2_done, y_done = (sem(n) for n in (
            "xt_done", "xh_done", "xl_done", "l1_done", "gelu_done", "hh_done", "hl_done", "l2_done", "y_done"))
        y_out = [sem("y_out0"), sem("y_out1")]
        goes_done = sem("goes_done")
        stored = sem("stored")

        block = ctx.enter_context(nc.Block())
        N_CONSTS = 15
        W_PARTS = 4
        W_COLS = 2 * E * FF // W_PARTS
        LOADS = 4
        SPL = B // LOADS

        @block.sync
        def _(sp):
            def load_x(i):
                sp.dma_start(acc[:, i * SPL * TPB:(i + 1) * SPL * TPB, :].rearrange("p (b j) d -> p b j d", j=TPB),
                             x_seq[:, i * SPL:(i + 1) * SPL]).then_inc(x_in[i], 16)
            load_x(0)
            load_x(1)
            sp.wait_ge(x_in[0], 16)
            load_x(2)
            load_x(3)
            sp.wait_ge(consts_in, 16 * N_CONSTS)
            sp.dma_start(wst[:, 0, :].rearrange("p (e f) -> p e f", e=E), W1.rearrange("e d f -> d e f")).then_inc(w_in, 16)
            sp.dma_start(wst[:, 1, :].rearrange("p (e c d) -> p e c d", e=E, c=CH),
                         W2.rearrange("e (c f) d -> f e c d", f=P)).then_inc(w_in, 16)
            sp.wait_ge(pool_const, 2)
            for t in range(T // U):
                sp.dma_start(b2diag[t * E:(t + 1) * E, t % TPB, :], b2).then_inc(b2_in, 16)
            sp.dma_start(grouped.rearrange("(p r) c -> p r c", p=P),
                         padrow[:, None, :].to_broadcast([P, ROWS // P, ROW])).then_inc(pads_out, 16)

            for b in range(B):
                sp.wait_ge(acc_done, b + 1)
                sp.dma_start(out_seq[:, b], acc[:, b * TPB:(b + 1) * TPB, :]).then_inc(stored, 16)

            sp.wait_ge(scattered[0], 16 * T)
            sp.wait_ge(scattered[1], 16 * T)
            sp.wait_ge(pads_out, 16)

            def load(k, q):
                j = k * U + q
                need(sp, goes_done, j - U + 1)
                need(sp, xt_done, j - U + 1)
                sp.dma_start(xs[q], grouped[bass.ds(j * TILE, TILE), :].rearrange("(h p) c -> p h c", p=P)
                             ).then_inc(xs_in[q], 16)
            steps(sp, N_TILES, load)

            sp.wait_ge(y_out[0], 16 * GROUPS * ((N_TILES + 1) // 2))
            sp.wait_ge(y_out[1], 16 * GROUPS * (N_TILES // 2))

        @block.gpsimd
        def _(pool):
            nc.gpsimd.memset(ident[:], 0.0)
            nc.gpsimd.memset(ones16[:], 1.0)
            nc.gpsimd.memset(zeros[:], 0.0)
            nc.gpsimd.memset(first_row[:], 0.0)
            nc.gpsimd.memset(minus_half[:], -0.5)
            nc.gpsimd.memset(padrow[:], 0.0)
            nc.gpsimd.iota(desc[:], pattern=[[-1, E]], base=E, channel_multiplier=0,
                           allow_small_or_imprecise_dtypes=True)
            nc.gpsimd.iota(jrow[:], pattern=[[1, N_TILES]], base=0, channel_multiplier=0,
                           allow_small_or_imprecise_dtypes=True)
            nc.gpsimd.memset(b2diag[:], 0.0).then_inc(pool_const, 1)
            pool.wait_ge(pool_const, 1)
            nc.gpsimd.memset(first_row[0:1, :], 1.0)
            nc.gpsimd.affine_select(out=ident[:], in_=ident[:], compare_op=ALU.not_equal, fill=1.0, base=0,
                                    pattern=[[-1, P]], channel_multiplier=1)
            nc.gpsimd.affine_select(out=before[:], in_=ones16[:], compare_op=ALU.is_gt, fill=0.0, base=0,
                                    pattern=[[1, P]], channel_multiplier=-1)
            nc.gpsimd.iota(padrow[:, D:D + 1].bitcast(I32), pattern=[[0, 1]], base=NOWHERE,
                           channel_multiplier=0).then_inc(pool_const, 1)
            pool.wait_ge(pool_const, 2)

            def first(k, q):
                t = bass.ds(k * U * TPB, U * TPB)
                pool.wait_ge(var_done, k + 1)
                nc.gpsimd.tensor_tensor(rstd[:, t], vare[:, t], minus_half[:], ALU.pow).then_inc(rstd_done, 1)

            def add_skipped(k, q):
                b = k * U + q
                ts = bass.ds(b * TPB, TPB)
                pool.wait_ge(skip_done, b + 1)
                pool.sem_inc(passed, 1)
                nc.gpsimd.tensor_tensor(acc[:, ts, :], acc[:, ts, :], skipped[q], ALU.add).then_inc(skipped_added, 1)
            first(0, 0)
            first(1, 0)
            add_skipped(0, 0)
            add_skipped(0, 1)
            first(2, 0)
            add_skipped(0, 2)
            add_skipped(0, 3)
            first(3, 0)
            steps(pool, B, add_skipped, done=U)

            pool.wait_ge(topsq_done, 1)
            nc.gpsimd.partition_all_reduce(maxsq[:], topsq[:], P, RMAX).then_inc(maxsq_done, 1)
            pool.wait_ge(b1max_done, 1)
            nc.gpsimd.partition_all_reduce(b1max[:], b1m[:], P, RMAX).then_inc(maxsq_done, 1)
            for i in range(W_PARTS):
                w, c = divmod(i, W_PARTS // 2)
                part = slice(c * W_COLS, (c + 1) * W_COLS)
                hi, lo = ((w1h, w1l), (w2h, w2l))[w]
                pool.wait_ge(w_high, i + 1)
                nc.gpsimd.tensor_tensor(lo[:, part], wst[:, w, part], hi[:, part], ALU.subtract).then_inc(w_low, 1)

            nc.gpsimd.iota(row[:, :, D].bitcast(I32).rearrange("p (b j) -> p b j", j=TPB),
                           pattern=[[SEQ, B], [1, TPB]], base=0, channel_multiplier=TPB).then_inc(dest_done, 1)
            pool.wait_ge(dest_done, 1)
            pool.wait_ge(pads_out, 16)
            for c in range(K):
                if c == 0:
                    pool.wait_ge(pos_ready, 1)
                else:
                    pool.wait_ge(scattered[0], 16 * T)
                    nc.gpsimd.tensor_copy(row[:, :, D + 1], gk[:, c, :]).then_inc(dest_done, 1)
                    pool.wait_ge(dest_done, 2)
                for t in range(T):
                    nc.gpsimd.indirect_dma_start(
                        grouped, bass.IndirectOffsetOnAxis(ap=pos[:, c, t:t + 1].bitcast(U32), axis=0),
                        row[:, t, :], None,
                        bounds_check=ROWS - 1, oob_is_err=False).then_inc(scattered[c], 16)

            pool.wait_ge(stored, 16 * B)

            def scatter(k, q):
                j, u = k * U + q, q % 2
                pool.wait_ge(y_done, j + 1)
                pool.wait_ge(goes_done, j + 1)
                need(pool, y_out[(q + 1) % 2], 16 * GROUPS * (2 * k + (q + 1) // 2))
                pool.sem_inc(passed, 1)
                for h in range(GROUPS):
                    nc.gpsimd.indirect_dma_start(
                        out, bass.IndirectOffsetOnAxis(ap=goes[:, q, h:h + 1].bitcast(U32), axis=0),
                        ysb[u][:, h, :], None, bounds_check=TOK - 1, oob_is_err=False, compute_op=ALU.add
                    ).then_inc(y_out[u], 16)
            steps(pool, N_TILES, scatter)

        @block.tensor
        def _(pe):
            pe.wait_ge(consts_in, 16 * N_CONSTS)
            pe.wait_ge(pool_const, 2)
            nc.tensor.transpose(ps[0:RANK, 0, 0:P], wdt1[:], ident[:])
            nc.tensor.transpose(ps[:, 1, 0:E * CH], b1rows[:], ident[0:E * CH, 0:E * CH]).then_inc(pe_setup, 1)
            pe.wait_ge(act_setup, 1)
            nc.tensor.matmul(ps[:, 2, 0:P], wdt1T[:], wdt2[:], start=True, stop=True)
            nc.tensor.matmul(ps[:, 3, 0:1], wdt2[:], cols[0:RANK, 2:3], start=True, stop=True).then_inc(pe_setup, 1)
            pe.wait_ge(act_setup, 4)

            def logits(k, q):
                b, u = k * U + q, q % 2
                pe.wait_ge(xnT2_done, b + 1)
                for j in range(TPB):
                    mm = nc.tensor.matmul(ps[:, 2, bass.ds((b * TPB + j) * E, E)], xnT2[:, u, j:SEQ:TPB], wG[:],
                                          start=True, stop=True, skip_group_check=True)
                mm.then_inc(logits_done, 1)

            def turn(k, q):
                b, u = k * U + q, q % 2
                need(pe, xnT_done, b - 1)
                pe.wait_ge(xn_done, TPB * (b + 1))
                for j in range(TPB):
                    mm = nc.tensor.transpose(ps[:, u, j * P:(j + 1) * P], xn2[:, u, j, :], ident[:])
                mm.then_inc(turned, 1)
                if isinstance(k, int) and k == 0 and q == 0:
                    return
                logits(*((k, q - 1) if q else (k - 1, U - 1)))
            steps(pe, B, turn)
            logits(B // U - 1, U - 1)

            pe.wait_ge(gate_mask, 1)
            nc.tensor.matmul(ps[:, 3, :], before[:], mask16[:].rearrange("p t e -> p (t e)"), start=True, stop=True)
            nc.tensor.matmul(ps[:, 4, :], ones16[:], mask16[:].rearrange("p t e -> p (t e)"), start=True, stop=True
                             ).then_inc(ranked, 1)
            def z(k, q):
                b, u = k * U + q, q % 2
                need(pe, relz_done, b - 1)
                need(pe, absz_done, b - 1)
                nc.tensor.matmul(ps[:, u, :], wdt[:], xnT[:, bass.ds(b, 1), :].rearrange("p a s -> p (a s)"),
                                 start=True, stop=True).then_inc(z_done, 1)
            pe.wait_ge(xnT_done, B)
            steps(pe, B, z)

            pe.wait_ge(p_ready, 1)
            for g in range(U):
                mm = nc.tensor.transpose(ps[:, 5, g * P:(g + 1) * P],
                                         gates[:, g * 16:(g + 1) * 16, :].rearrange("p t e -> p (t e)"), ident[:])
            mm.then_inc(p_turned, 1)
            pe.wait_ge(pT_done, 1)

            pe.wait_ge(b2_in, 16 * (T // U))
            pe.wait_ge(skipped_added, B)
            pe.wait_ge(pos_ready, 1)

            def project(k, q):
                b, u = k * U + q, q % 2
                need(pe, acc_done, b - 1)
                if q == 0:
                    pe.wait_ge(pTs_done, k + 1)
                bank = ps[:, 6 + u, :]
                rows = slice(q * TPB * E, (q + 1) * TPB * E)
                nc.tensor.matmul(bank, pTs[rows, :], b2diag[rows].rearrange("p j d -> p (j d)"),
                                 start=True, stop=False, skip_group_check=True)
                nc.tensor.matmul(bank, first_row[:], bout[:, None, :].to_broadcast([P, TPB, D]),
                                 start=False, stop=False, skip_group_check=True)
                nc.tensor.matmul(bank, ident[:], acc[:, bass.ds(b * TPB, TPB), :].rearrange("p j d -> p (j d)"),
                                 start=False, stop=False, skip_group_check=True)
                pe.wait_ge(ret_done, b + 1)
                for j in range(TPB):
                    mm = nc.tensor.matmul(ps[:, 6 + u, j * D:(j + 1) * D], ret[:, u, j:SEQ:TPB], wO[:],
                                          start=False, stop=(j == TPB - 1), skip_group_check=True)
                mm.then_inc(out_done, 1)

            def write_read(k, q):
                b, u = k * U + q, q % 2
                need(pe, content_done, b - 1)
                need(pe, ret_done, b - 1)
                xb = xnT[:, bass.ds(b, 1), :].rearrange("p a s -> p (a s)")
                nc.tensor.matmul(ps[:, 2 + u, :], wB[:], xb, start=True, stop=True)
                nc.tensor.matmul(ps[:, 4 + u, :], wC[:], xb, start=True, stop=True).then_inc(bc_done, 1)
                if isinstance(k, int) and k == 0 and q == 0:
                    return
                project(*((k, q - 1) if q else (k - 1, U - 1)))
            steps(pe, B, write_read)

            def turn_tile(k, q):
                j, u = k * U + q, q % 2
                pe.wait_ge(xs_in[q], 16 * (k + 1))
                for h in range(GROUPS):
                    mm = nc.tensor.transpose(ps[:, u, h * P:(h + 1) * P], xs[q][:, h, 0:D], ident[:])
                mm.then_inc(xt_done, 1)

            def weights_of(k, q):
                return pe.value_load(tile_column[0:1, bass.ds(k * U + q, 1)], min_val=0, max_val=(E - 1) * FF)

            def layer1(k, q, w0):
                j, u = k * U + q, q % 2
                pe.wait_ge(xl_done, j + 1)
                need(pe, gelu_done, CH * j)
                for c in range(CH):
                    o = ps[:, 2 + c, :]
                    hi, lo = (w[:, bass.ds(w0 + c * P, P)] for w in (w1h, w1l))
                    nc.tensor.matmul(o, hi, xh[q], start=True, stop=False)
                    nc.tensor.matmul(o, hi, xl[q], start=False, stop=False)
                    nc.tensor.matmul(o, lo, xh[q], start=False, stop=True).then_inc(l1_done, 1)

            def layer2(k, q, w0):
                j, u = k * U + q, q % 2
                pe.wait_ge(hl_done, CH * (j + 1))
                for h in range(GROUPS):
                    o = ps[:, 6 + u, h * D:(h + 1) * D]
                    for c in range(CH):
                        hi, lo = (w[:, bass.ds(w0 + c * D, D)] for w in (w2h, w2l))
                        a, b = (v[u][:, c, h * P:(h + 1) * P] for v in (hh, hl))
                        nc.tensor.matmul(o, a, hi, start=(c == 0), stop=False, skip_group_check=True)
                        nc.tensor.matmul(o, a, lo, start=False, stop=False, skip_group_check=True)
                        mm = nc.tensor.matmul(o, b, hi, start=False, stop=(c == CH - 1), skip_group_check=True)
                mm.then_inc(l2_done, 1)

            column = [None, None]

            def tile_step(k, q):
                if q == 0:
                    column[1] = weights_of(k, 0)
                layer1(k, q, column[1])
                if q == 0 and not (isinstance(k, int) and k == 0):
                    column[0] = weights_of(k - 1, U - 1)
                last = q + 1 == U or isinstance(k, int) and k * U + q + 1 == N_TILES
                next_column = None if last else weights_of(k, q + 1)
                if not (isinstance(k, int) and k * U + q + 2 >= N_TILES):
                    turn_tile(*((k, q + 2) if q + 2 < U else (k + 1, q + 2 - U)))
                if not (isinstance(k, int) and k == 0 and q == 0):
                    layer2(*((k, q - 1) if q else (k - 1, U - 1)), column[0])
                column[:] = column[1], next_column
            project(B // U - 1, U - 1)
            turn_tile(0, 0)
            turn_tile(0, 1)
            pe.wait_ge(w_low, W_PARTS)
            pe.wait_ge(w_high, W_PARTS)
            pe.wait_ge(tile_ready, 1)
            steps(pe, N_TILES, tile_step)
            layer2((N_TILES - 1) // U, (N_TILES - 1) % U, column[0])

        @block.scalar
        def _(act):
            def col(i, v, n=P):
                act.dma_start(cols[0:n, i:i + 1], v.rearrange("(a b) -> a b", b=1)).then_inc(consts_in, 16)
            for i, v, n in ((0, b_B, P), (1, b_C, P), (2, b_dt1, RANK), (3, b_dt2, P), (4, omega, P)):
                col(i, v, n)
            for dst, src in ((wB, W_B), (wC, W_C), (wO, W_out), (wG, Wg), (wdt1, W_dt1), (wdt2, W_dt2)):
                act.dma_start(dst[:], src).then_inc(consts_in, 16)
            act.dma_start(b1rows[:], b1.rearrange("e (c f) -> (e c) f", f=P)).then_inc(consts_in, 16)
            act.dma_start(bout[:], b_out.partition_broadcast(P)).then_inc(consts_in, 16)
            act.dma_start(skip[:], D_skip.partition_broadcast(P)).then_inc(consts_in, 16)
            act.dma_start(bgate[:], bg.partition_broadcast(P)).then_inc(consts_in, 16)
            act.wait_ge(pe_setup, 1)
            nc.scalar.copy(wdt1T[:], ps[0:RANK, 0, 0:P]).then_inc(act_setup, 1)
            nc.scalar.copy(b1T[:], ps[:, 1, 0:E * CH]).then_inc(act_setup, 1)
            act.wait_ge(pe_setup, 2)
            nc.scalar.copy(wdt[:], ps[:, 2, 0:P]).then_inc(act_setup, 1)
            nc.scalar.activation(cols[:, 5:6], ps[:, 3, 0:1], ACT.Identity, bias=cols[:, 3:4]).then_inc(act_setup, 1)

            def keep(k, q):
                b, u = k * U + q, q % 2
                act.wait_ge(turned, b + 1)
                need(act, logits_done, b - 1)
                nc.scalar.copy(row[:, bass.ds(b * TPB, TPB), 0:D], xn2[:, u]).then_inc(row_done, 1)
                t = ps[:, u, :].rearrange("p (j n) -> p n j", j=TPB)
                nc.scalar.copy(xnT2[:, u, :].rearrange("p (n j) -> p n j", j=TPB), t).then_inc(xnT2_done, 1)
                nc.scalar.copy(xnT[:, bass.ds(b, 1), :].rearrange("p a (n j) -> p (a n) j", j=TPB), t
                               ).then_inc(xnT_done, 1)
                if not (isinstance(k, int) and k == 0):
                    square((k - 1) * (U + 1) + q)
                    if q == U - 1:
                        square((k - 1) * (U + 1) + U)

            def square(piece):
                nc.scalar.activation(squares[:, bass.ds(piece, 1), :].rearrange("p a n -> p (a n)"),
                                     shared[:, bass.ds(piece * SEQ, SEQ)], ACT.Square,
                                     accum_out=sumsq[:, bass.ds(piece, 1)]).then_inc(sumsq_done, 1)

            def weights_in():
                act.wait_ge(w_in, 32)
            steps(act, B, keep, between=weights_in)
            square(B - 1)

            act.wait_ge(gate_max, 1)
            nc.scalar.activation(pr[:], lg[:], ACT.Exp).then_inc(gate_exp, 1)
            act.wait_ge(scales_done, 1)
            act.wait_ge(sumsq_done, B)
            for i in range(W_PARTS):
                w, c = divmod(i, W_PARTS // 2)
                part = slice(c * W_COLS, (c + 1) * W_COLS)
                nc.scalar.activation(wst[:, w, part], wst[:, w, part], ACT.Copy, scale=scl[:, w:w + 1]
                                     ).then_inc(w_scaled, 1)
                act.wait_ge(w_scaled, i + 1)
                nc.scalar.copy((w1h, w2h)[w][:, part], wst[:, w, part]).then_inc(w_high, 1)

            nc.scalar.preload_act_table_set("natural_log_exp_and_others")
            act.wait_ge(counts_used, 1)

            def softplus(k, q):
                b, u = k * U + q, q % 2
                act.wait_ge(z_done, b + 1)
                need(act, exp_done, b - 1)
                nc.scalar.activation(absz[:, u, :], ps[:, u, :], ACT.Abs, bias=cols[:, 5:6]).then_inc(absz_done, 1)
                need(act, sum_done, b - 1)
                nc.scalar.activation(relz[:, u, :], ps[:, u, :], ACT.Relu, bias=cols[:, 5:6]).then_inc(relz_done, 1)
                act.wait_ge(absz_done, b + 1)
                need(act, ln_done, b - 1)
                nc.scalar.activation(ex[:, u, :], absz[:, u, :], ACT.Exp, scale=-1.0).then_inc(exp_done, 1)
                act.wait_ge(exp_done, b + 1)
                nc.scalar.activation(lnz[:, u, :], ex[:, u, :], ACT.Ln, bias=1.0).then_inc(ln_done, 1)
            steps(act, B, softplus)

            act.wait_ge(p_turned, 1)
            nc.scalar.copy(pT[:].rearrange("p g n -> p (g n)"), ps[:, 5, :]).then_inc(pT_done, 1)

            nc.scalar.preload_act_table(ACT.Sin)

            def waves(k, q):
                b, u = k * U + q, q % 2
                act.wait_ge(phase_done, b + 1)
                need(act, q2_done, b - 1)
                need(act, q1_done, b - 1)
                f = phase[:, bass.ds(b, 1), :].rearrange("p a s -> p (a s)")
                nc.scalar.activation(sn[:, u, :], f, ACT.Sin, scale=TWO_PI).then_inc(sin_done, 1)
                nc.scalar.activation(ab[:, u, :], f, ACT.Abs).then_inc(ab_done, 1)
                act.wait_ge(ab_done, b + 1)
                nc.scalar.activation(cs[:, u, :], ab[:, u, :], ACT.Sin, scale=-TWO_PI, bias=cols[:, 7:8]
                                     ).then_inc(cos_done, 1)
                if q == 0:
                    need(act, out_done, b)
                    nc.scalar.copy(pTs[:], pT[:, bass.ds(k, 1), :].rearrange("p a n -> p (a n)")).then_inc(pTs_done, 1)
                if not (isinstance(k, int) and k == 0 and q == 0):
                    keep_out(*((k, q - 1) if q else (k - 1, U - 1)))

            def keep_out(k, q):
                b, u = k * U + q, q % 2
                act.wait_ge(out_done, b + 1)
                nc.scalar.copy(acc[:, bass.ds(b * TPB, TPB), :].rearrange("p j d -> p (j d)"), ps[:, 6 + u, :]
                               ).then_inc(acc_done, 1)
            act.wait_ge(sum_done, B)
            act.wait_ge(ln_done, B)
            act.wait_ge(pT_done, 1)
            steps(act, B, waves)

            nc.scalar.preload_act_table(ACT.Gelu)
            act.wait_ge(ab_done, B)
            act.wait_ge(cos_done, B)
            act.wait_ge(sin_done, B)

            def high(k, q):
                j, u = k * U + q, q % 2
                act.wait_ge(xt_done, j + 1)
                need(act, l1_done, CH * (j - 3))
                nc.scalar.copy(xh[q], ps[:, u, 0:TILE]).then_inc(xh_done, 1)

            def gelu(k, q):
                j, u = k * U + q, q % 2
                e = act.value_load(tile_expert[0:1, bass.ds(j, 1)], min_val=0, max_val=E - 1)
                need(act, hl_done, CH * (j - 1))
                for c in range(CH):
                    act.wait_ge(l1_done, CH * j + c + 1)
                    nc.scalar.activation(gel[u][:, c, :], ps[:, 2 + c, :],
                                         ACT.Gelu, bias=b1T[:, bass.ds(e * CH + c, 1)], scale=scl[:, 2:3]
                                         ).then_inc(gelu_done, 1)

            def result(k, q):
                j, u = k * U + q, q % 2
                act.wait_ge(l2_done, j + 1)
                need(act, y_out[u], 16 * GROUPS * (2 * k + q // 2))
                for h in range(GROUPS):
                    y = nc.scalar.activation(ysb[u][:, h, :], ps[:, 6 + u, h * D:(h + 1) * D], ACT.Copy,
                                             scale=scale_y[:, q, h:h + 1])
                y.then_inc(y_done, 1)

            def tile_step(k, q):
                gelu(k, q)
                if not (isinstance(k, int) and k * U + q + 2 >= N_TILES):
                    high(*((k, q + 2) if q + 2 < U else (k + 1, q + 2 - U)))
                if not (isinstance(k, int) and k == 0 and q == 0):
                    result(*((k, q - 1) if q else (k - 1, U - 1)))
            act.wait_ge(tile_ready, 1)
            keep_out(B // U - 1, U - 1)
            high(0, 0)
            high(0, 1)
            steps(act, N_TILES, tile_step)
            result((N_TILES - 1) // U, (N_TILES - 1) % U)

        @block.vector
        def _(dve):
            def norm(k, q):
                b, u = k * U + q, q % 2
                need(dve, row_done, b - 1)
                need(dve, turned, b - 1)
                need(dve, skip_done, b - 1)
                dve.wait_ge(rstd_done, k + 1)
                for j in range(TPB):
                    t = b * TPB + j
                    nc.vector.tensor_scalar(xn2[:, u, j, :], acc[:, bass.ds(t, 1), :].rearrange("p a d -> p (a d)"),
                                            mean[:, bass.ds(t, 1)], rstd[:, bass.ds(t, 1)], ALU.subtract, ALU.mult
                                            ).then_inc(xn_done, 1)
                need(dve, skipped_added, b - U + 1)
                dve.wait_ge(xn_done, TPB * (b + 1))
                nc.vector.tensor_tensor(skipped[q], xn2[:, u], skip[:, None, :].to_broadcast([P, TPB, D]), ALU.mult
                                        ).then_inc(skip_done, 1)

            def moments(k, _):
                dve.wait_ge(x_in[k], 16)
                for i in range(U * TPB):
                    t = k * U * TPB + i
                    mm = nc.vector.bn_stats(stats[:, bass.ds(t, 1), :].rearrange("p a c -> p (a c)"),
                                            acc[:, bass.ds(t, 1), :].rearrange("p a d -> p (a d)"))
                mm.then_inc(stats_done, 1)
                dve.wait_ge(stats_done, k + 1)
                ts = bass.ds(k * U * TPB, U * TPB)
                m_even, s_even, m_odd, s_odd = (stats[:, ts, i:i + 1].rearrange("p t a -> p (t a)") for i in (1, 2, 4, 5))
                nc.vector.tensor_tensor(mean[:, ts], m_even, m_odd, ALU.add)
                nc.vector.tensor_tensor(gap[:, ts], m_even, m_odd, ALU.subtract)
                nc.vector.tensor_tensor(vare[:, ts], s_even, s_odd, ALU.add).then_inc(moment, 1)
                dve.wait_ge(moment, 2 * k + 1)
                nc.vector.tensor_scalar(mean[:, ts], mean[:, ts], 0.5, None, ALU.mult)
                nc.vector.tensor_scalar(vare[:, ts], vare[:, ts], 1.0 / D, 1e-5, ALU.mult, ALU.add)
                nc.vector.scalar_tensor_tensor(out=gap[:, ts], in0=gap[:, ts], scalar=0.25, in1=gap[:, ts],
                                               op0=ALU.mult, op1=ALU.mult).then_inc(moment, 1)
                dve.wait_ge(moment, 2 * k + 2)
                nc.vector.tensor_tensor(vare[:, ts], vare[:, ts], gap[:, ts], ALU.add).then_inc(var_done, 1)

            moments(0, 0)
            moments(1, 0)
            dve.wait_ge(consts_in, 16 * N_CONSTS)
            norm(0, 0)
            norm(0, 1)
            moments(2, 0)
            norm(0, 2)
            norm(0, 3)
            moments(3, 0)
            steps(dve, B, norm, done=U)

            V = nc.vector

            n_gate = [0]

            def link(ins):
                n_gate[0] += 1
                ins.then_inc(gate, 1)
                dve.wait_ge(gate, n_gate[0])

            def over_e(v):
                return v[:, :, None].to_broadcast([P, T, E])

            dve.wait_ge(act_setup, 4)
            V.tensor_reduce(b1m[:], b1T[:], AX, ALU.max, apply_absolute_value=True).then_inc(b1max_done, 1)
            dve.wait_ge(sumsq_done, B)
            V.tensor_reduce(topsq[:], sumsq[:].rearrange("p (w n) -> p w n", w=2), AX, ALU.max).then_inc(topsq_done, 1)
            dve.wait_ge(logits_done, B)
            dve.wait_ge(skipped_added, B)
            dve.wait_ge(pool_const, 2)
            dve.wait_ge(consts_in, 16 * N_CONSTS)
            link(V.memset(cols[:, 7:8], 1.5707963))
            link(V.tensor_scalar(cols[:, 6:7], cols[:, 4:5], 1.0 / 6.283185307179586, None, ALU.mult))
            link(V.tensor_tensor(lg[:], ps[:, 2, :].rearrange("p (t e) -> p t e", e=E),
                                 bgate[:, None, :].to_broadcast([P, T, E]), ALU.add))
            link(V.tensor_reduce(mx[:], lg[:], AX, ALU.max))
            V.tensor_tensor(lg[:], lg[:], over_e(mx[:]), ALU.subtract).then_inc(gate_max, 1)

            n_scale = [0]

            def scale(ins):
                n_scale[0] += 1
                ins.then_inc(scale_step, 1)
                dve.wait_ge(scale_step, n_scale[0])

            dve.wait_ge(maxsq_done, 2)
            scale(V.tensor_scalar(maxsq[:], maxsq[:], 2.0 ** -100, 2.0 ** 100, ALU.max, ALU.min))
            scale(V.tensor_scalar(pwi, maxsq[:].bitcast(I32), 23, None, ALU.logical_shift_right))
            scale(V.tensor_scalar(pwi, pwi, 129, None, ALU.add))
            scale(V.tensor_scalar(pwi, pwi, 1, 23, ALU.logical_shift_right, ALU.logical_shift_left))
            scale(V.scalar_tensor_tensor(out=pw[:, 2:3], in0=pw[:, 0:1], scalar=2048.0, in1=b1max[:],
                                         op0=ALU.mult, op1=ALU.add))
            scale(V.tensor_scalar(pw[:, 3:4].bitcast(I32), pw[:, 2:3].bitcast(I32), 0x7F800000, None, ALU.bitwise_and))
            scale(V.reciprocal(scl[:, 5:7], pw[:, 0:2]))
            scale(V.reciprocal(scl[:, 7:8], pw[:, 3:4]))
            scale(V.tensor_scalar(scl[:, 0:2], scl[:, 5:7], 2.0 ** 15, None, ALU.mult))
            scale(V.tensor_scalar(scl[:, 2:3], pw[:, 0:1], 2.0 ** -15, None, ALU.mult))
            scale(V.tensor_scalar(scl[:, 3:4], scl[:, 7:8], 2.0 ** 14, None, ALU.mult))
            V.scalar_tensor_tensor(out=scl[:, 4:5], in0=pw[:, 3:4], scalar=2.0 ** -29, in1=pw[:, 1:2],
                                   op0=ALU.mult, op1=ALU.mult).then_inc(scales_done, 1)

            dve.wait_ge(gate_exp, 1)
            link(V.tensor_reduce(sm[:], pr[:], AX, ALU.add))
            link(V.reciprocal(sm[:], sm[:]))
            link(V.tensor_tensor(pr[:], pr[:], over_e(sm[:]), ALU.mult))
            rest = pr
            for c, one_hot in ((0, g1), (1, g2)):
                link(V.tensor_reduce(m12[:, c, :], rest[:], AX, ALU.max))
                link(V.tensor_tensor(one_hot[:], rest[:], over_e(m12[:, c, :]), ALU.is_equal))
                link(V.tensor_tensor(one_hot[:], one_hot[:], desc[:, None, :].to_broadcast([P, T, E]), ALU.mult))
                link(V.tensor_reduce(mx[:], one_hot[:], AX, ALU.max))
                link(V.tensor_tensor(one_hot[:], one_hot[:], over_e(mx[:]), ALU.is_equal))
                if c == 0:
                    rest = lg
                    link(V.scalar_tensor_tensor(out=lg[:].rearrange("p t e -> p (t e)"),
                                                in0=g1[:].rearrange("p t e -> p (t e)"), scalar=-2.0,
                                                in1=pr[:].rearrange("p t e -> p (t e)"), op0=ALU.mult, op1=ALU.add))
            V.tensor_tensor(mask16[:], g1[:], g2[:], ALU.add).then_inc(gate_mask, 1)
            dve.wait_ge(gate_mask, 1)
            link(V.tensor_tensor(den[:], m12[:, 0, :], m12[:, 1, :], ALU.add))
            link(V.tensor_scalar(den0[:], den[:], 0.0, None, ALU.is_equal))
            link(V.tensor_tensor(den[:], den[:], den0[:], ALU.add))
            link(V.reciprocal(den[:], den[:]))
            link(V.tensor_tensor(gk[:, 0, :], m12[:, 0, :], den[:], ALU.mult))
            link(V.tensor_tensor(gk[:, 1, :], m12[:, 1, :], den[:], ALU.mult))
            dve.wait_ge(row_done, B)
            link(V.tensor_copy(row[:, :, D + 1], gk[:, 0, :]))

            dve.wait_ge(ranked, 1)
            dve.wait_ge(row_done, B)
            dve.wait_ge(turned, B)
            link(V.tensor_copy(tot, ps[:, 4, :].rearrange("p (t e) -> p e t", e=E)))
            for e in range(E):
                i = V.tensor_tensor_scan(cum[:, e, :], tot[:, e, :], zeros[:, 0:T], 0.0, ALU.add, ALU.add)
            link(i)
            count, tiles, ends, start = (sizes[:, i, :] for i in range(4))
            link(V.tensor_copy(count, cum[:, :, T - 1]))
            link(V.tensor_scalar(tiles, count, 1.0 / TILE, (TILE - 1.0) / TILE - 0.5 + 0.5 / TILE, ALU.mult, ALU.add))
            link(V.tensor_scalar(tiles, tiles, ROUND, None, ALU.add))
            link(V.tensor_scalar(tiles, tiles, ROUND, None, ALU.subtract))
            link(V.tensor_tensor_scan(ends, tiles, zeros[:, 0:E], 0.0, ALU.add, ALU.add))
            link(V.tensor_tensor(start, ends, tiles, ALU.subtract))
            link(V.tensor_scalar(start, start, float(TILE), None, ALU.mult))
            link(V.tensor_tensor(cum, cum, tot, ALU.subtract))
            link(V.tensor_tensor(cum, cum, start[:, :, None].to_broadcast([P, E, T]), ALU.add))
            V.tensor_tensor(lg[:], ps[:, 3, :].rearrange("p (t e) -> p t e", e=E),
                            cum.rearrange("p e t -> p t e"), ALU.add).then_inc(counts_used, 1)
            dve.wait_ge(counts_used, 1)
            for c, one_hot in ((0, g1), (1, g2)):
                link(V.tensor_tensor(one_hot[:], one_hot[:], lg[:], ALU.mult))
                link(V.tensor_reduce(posf[:, c, :], one_hot[:], AX, ALU.add))
            V.tensor_copy(pos[:], posf[:]).then_inc(pos_ready, 1)
            link(V.tensor_tensor(past, jrow[:, :, None].to_broadcast([P, N_TILES, E]),
                                 ends[:, None, :].to_broadcast([P, N_TILES, E]), ALU.is_ge))
            link(V.tensor_reduce(tile_e[:], past, AX, ALU.add))
            V.tensor_scalar(tile_expert[:], tile_e[:], float(E - 1), None, ALU.min)
            V.tensor_scalar(tile_column[:], tile_e[:], float(E - 1), float(FF), ALU.min, ALU.mult).then_inc(tile_ready, 1)

            link(V.tensor_tensor(pr[:], pr[:], mask16[:], ALU.mult))
            V.tensor_tensor(gates[:], pr[:], over_e(den[:]), ALU.mult).then_inc(p_ready, 1)

            w_turn = cols[:, 6:7]

            def total(k, q):
                b, u = k * U + q, q % 2
                dve.wait_ge(ln_done, b + 1)
                dve.wait_ge(relz_done, b + 1)
                need(dve, phase_done, b - 1)
                V.tensor_tensor_scan(steps_sum[u], relz[:, u, :], lnz[:, u, :], 0.0, ALU.add, ALU.add
                                     ).then_inc(sum_done, 1)

            def to_phase(k, q):
                b, u = k * U + q, q % 2
                dve.wait_ge(sum_done, b + 1)
                need(dve, t2, b)
                V.tensor_scalar(turns, steps_sum[u], w_turn, ROUND, ALU.mult, ALU.add).then_inc(t1, 1)
                if not (isinstance(k, int) and k * U + q + 1 == B):
                    total(*((k, q + 1) if q + 1 < U else (k + 1, 0)))
                dve.wait_ge(t1, b + 1)
                need(dve, phase_done, b)
                V.tensor_scalar(whole, turns, ROUND, None, ALU.subtract).then_inc(t2, 1)
                dve.wait_ge(t2, b + 1)
                V.scalar_tensor_tensor(out=phase[:, bass.ds(b, 1), :].rearrange("p a s -> p (a s)"),
                                       in0=steps_sum[u], scalar=w_turn, in1=whole, op0=ALU.mult, op1=ALU.subtract
                                       ).then_inc(phase_done, 1)

            dve.wait_ge(p_ready, 1)
            dve.wait_ge(w_low, W_PARTS)
            total(0, 0)
            for j in range(U):
                to_phase(0, j)
            with dve.Fori(1, B // U - 1) as k:
                for q in range(U):
                    to_phase(k, q)
            for j in range(U):
                to_phase(B // U - 1, j)

            def write(k, q):
                b, u = k * U + q, q % 2
                xb = xnT[:, bass.ds(b, 1), :].rearrange("p a s -> p (a s)")
                dve.wait_ge(bc_done, b + 1)
                V.scalar_tensor_tensor(out=content, in0=ps[:, 2 + u, :], scalar=cols[:, 0:1], in1=xb,
                                       op0=ALU.add, op1=ALU.mult).then_inc(content_done, 1)

            def recall(k, q):
                b, u = k * U + q, q % 2
                dve.wait_ge(content_done, b + 1)
                dve.wait_ge(cos_done, b + 1)
                V.tensor_tensor(p1, content, cs[:, u, :], ALU.mult).then_inc(p1_done, 1)
                V.tensor_tensor(p2, content, sn[:, u, :], ALU.mult).then_inc(p2_done, 1)
                dve.wait_ge(p1_done, b + 1)
                need(dve, ret_done, b)
                V.tensor_tensor_scan(m1, p1, zeros[:], 0.0, ALU.add, ALU.add).then_inc(m1_done, 1)
                dve.wait_ge(p2_done, b + 1)
                V.tensor_tensor_scan(m2, p2, zeros[:], 0.0, ALU.add, ALU.add).then_inc(m2_done, 1)
                dve.wait_ge(m1_done, b + 1)
                V.tensor_tensor(q1, m1, cs[:, u, :], ALU.mult).then_inc(q1_done, 1)
                dve.wait_ge(m2_done, b + 1)
                V.tensor_tensor(q2, m2, sn[:, u, :], ALU.mult).then_inc(q2_done, 1)
                if not (isinstance(k, int) and k * U + q + 1 == B):
                    write(*((k, q + 1) if q + 1 < U else (k + 1, 0)))
                dve.wait_ge(q2_done, b + 1)
                dve.wait_ge(q1_done, b + 1)
                V.tensor_tensor(qs, q1, q2, ALU.add).then_inc(qs_done, 1)
                dve.wait_ge(qs_done, b + 1)
                need(dve, out_done, b - 1)
                V.scalar_tensor_tensor(out=ret[:, u, :], in0=ps[:, 4 + u, :], scalar=cols[:, 1:2], in1=qs,
                                       op0=ALU.add, op1=ALU.mult).then_inc(ret_done, 1)
            dve.wait_ge(phase_done, B)
            dve.wait_ge(p_turned, 1)
            write(0, 0)
            for j in range(U):
                recall(0, j)
            with dve.Fori(1, B // U - 1) as k:
                for q in range(U):
                    recall(k, q)
            for j in range(U):
                recall(B // U - 1, j)

            def low(k, q):
                j, u = k * U + q, q % 2
                dve.wait_ge(xh_done, j + 1)
                need(dve, l1_done, CH * (j - 3))
                V.tensor_tensor(xl[q], ps[:, u, 0:TILE], xh[q], ALU.subtract).then_inc(xl_done, 1)

            def keep_goes(k, q):
                dve.wait_ge(xs_in[q], 16 * (k + 1))
                need(dve, y_out[q % 2], 16 * GROUPS * (2 * k + q // 2 - 1))
                V.tensor_scalar(scale_y[:, q, :], xs[q][:, :, D + 1], scl[:, 4:5], None, ALU.mult)
                V.tensor_copy(goes[:, q, :], xs[q][:, :, D].bitcast(I32)).then_inc(goes_done, 1)

            def hidden(k, q):
                j, u = k * U + q, q % 2
                need(dve, l2_done, j - 1)
                for c in range(CH):
                    dve.wait_ge(gelu_done, CH * j + c + 1)
                    g, a, b = (v[u][:, c, :] for v in (gel, hh, hl))
                    V.tensor_scalar(a, g, scl[:, 3:4], None, ALU.mult).then_inc(hh_done, 1)
                    dve.wait_ge(hh_done, CH * j + c + 1)
                    V.scalar_tensor_tensor(out=b, in0=g, scalar=scl[:, 3:4], in1=a, op0=ALU.mult, op1=ALU.subtract
                                           ).then_inc(hl_done, 1)

            def tile_step(k, q):
                if not (isinstance(k, int) and k * U + q + 1 >= N_TILES):
                    keep_goes(*((k, q + 1) if q + 1 < U else (k + 1, 0)))
                hidden(k, q)
                if not (isinstance(k, int) and k * U + q + 2 >= N_TILES):
                    low(*((k, q + 2) if q + 2 < U else (k + 1, q + 2 - U)))
            low(0, 0)
            low(0, 1)
            keep_goes(0, 0)
            steps(dve, N_TILES, tile_step)


_INS = ["x", "W_B", "b_B", "W_C", "b_C", "W_dt1", "b_dt1", "W_dt2", "b_dt2", "omega_base", "D", "W_out", "b_out"]
_FFN = ["W1", "b1", "W2", "b2", "Wg", "bg"]


def kernel(**inputs):
    import numpy as np
    import concourse.bacc as bacc
    from concourse import mybir as _mybir
    from concourse.bass_utils import run_bass_kernel_spmd

    nc = bacc.Bacc("TRN2", target_bir_lowering=False, num_devices=1)
    arrays, args = {}, []
    for name in ["L0_attn_" + n for n in _INS] + ["L0_ffn_" + n for n in _FFN]:
        a = np.ascontiguousarray(inputs[name])
        if name == "L0_attn_x":
            a = a.reshape(TOK, D)
        arrays["in_" + name] = a
        args.append(nc.dram_tensor("in_" + name, a.shape, _mybir.dt.from_np(a.dtype), kind="ExternalInput").ap())
    out = nc.dram_tensor("out_0", (TOK, D), F32, kind="ExternalOutput").ap()
    program(nc, *args, out)
    r = run_bass_kernel_spmd(nc, [arrays], core_ids=[0])
    return r.results[0]["out_0"].reshape(B, SEQ, D)
```
